# Optimizing a Trainium2 kernel written in Bass

```python
import numpy as np
import jax
import jax.numpy as jnp

def _softmax(x, axis=-1):
    return jax.nn.softmax(x, axis=axis)

def _gelu(x):
    return jax.nn.gelu(x, approximate=True)

def _silu(x):
    return jax.nn.silu(x)

def _sigmoid(x):
    return jax.nn.sigmoid(x)

def _layernorm(x, axis=-1, eps=1e-05):
    m = jnp.mean(x, axis=axis, keepdims=True)
    v = jnp.var(x, axis=axis, keepdims=True)
    return (x - m) / jnp.sqrt(v + eps)

def _scatter_add(tgt, idx, src, axis=0):
    return tgt.at[idx].add(src)

def _segment_sum(src, seg, n):
    return jax.ops.segment_sum(src, seg, n)
kernel_name = 'mk_flamingo_gated_d1_seqx_r8_36f369'

def setup_inputs(seed: int=0):
    np.random.seed(seed)
    _w = jnp.asarray

    def _rec_inputs():
        import jax
        import jax.numpy as jnp
        _rk = jax.random.key(seed)
        x = 0.0002417 + 0.9998 * jax.random.normal(jax.random.fold_in(_rk, 1), (16, 256, 128), jnp.float32)
        _lenS = 256 - jax.random.randint(jax.random.fold_in(_rk, 7), (16,), 0, max(1, 256 // 4) + 1, jnp.int32)
        _lenS2 = 1601 - jax.random.randint(jax.random.fold_in(_rk, 8), (16,), 0, max(1, 1601 // 4) + 1, jnp.int32)
        _ctx_1024P = jax.random.normal(jax.random.fold_in(_rk, 11), (16, 16, 128), jnp.float32)
        _ctx_1024c = jax.random.dirichlet(jax.random.fold_in(_rk, 511), 0.3 * jnp.ones((16,), jnp.float32), (16, 1601))
        _ctx_1024t = jnp.einsum('bsk,bkd->bsd', _ctx_1024c, _ctx_1024P)
        _ctx_1024t = _ctx_1024t * jax.lax.rsqrt(jnp.mean(jnp.square(_ctx_1024t)) + 1e-12) * 0.953939
        ctx_1024 = 7.22013e-05 + 1.00017 * (_ctx_1024t + 0.3 * jax.random.normal(jax.random.fold_in(_rk, 611), (16, 1601, 128), jnp.float32))
        _g = jax.random.normal(jax.random.fold_in(_rk, 9001), (2, 1), jnp.float32)
        _g = jnp.sign(_g) * jnp.maximum(jnp.abs(_g), 1.0) + (_g == 0) * 1.0
        g_xattn = _g[0]
        g_ffn = _g[1]
        return (x, ctx_1024, g_xattn, g_ffn)
    x, ctx_1024, g_xattn, g_ffn = _rec_inputs()

    def _L0_xattn_setup():
        import jax, jax.numpy as jnp
        import numpy as np
        D_MODEL = 128
        NUM_HEADS = 16
        DEPTH = D_MODEL // NUM_HEADS

        def _split_heads(x):
            B, S, _ = x.shape
            return x.reshape(B, S, NUM_HEADS, DEPTH).transpose(0, 2, 1, 3)
        key = jax.random.key(seed)
        ks = jax.random.split(key, 11)
        B, S = (4, 256)
        scale = 1.0 / np.sqrt(D_MODEL)
        inp = {'v': jax.random.normal(ks[0], (B, S, D_MODEL), jnp.float32), 'k': jax.random.normal(ks[1], (B, S, D_MODEL), jnp.float32), 'q': jax.random.normal(ks[2], (B, S, D_MODEL), jnp.float32), 'wq_w': jax.random.normal(ks[3], (D_MODEL, D_MODEL), jnp.float32) * scale, 'wq_b': jnp.zeros((D_MODEL,), jnp.float32), 'wk_w': jax.random.normal(ks[4], (D_MODEL, D_MODEL), jnp.float32) * scale, 'wk_b': jnp.zeros((D_MODEL,), jnp.float32), 'wv_w': jax.random.normal(ks[5], (D_MODEL, D_MODEL), jnp.float32) * scale, 'wv_b': jnp.zeros((D_MODEL,), jnp.float32), 'dense_w': jax.random.normal(ks[6], (D_MODEL, D_MODEL), jnp.float32) * scale, 'dense_b': jnp.zeros((D_MODEL,), jnp.float32)}
        return inp
    _L0_xattn_all = _L0_xattn_setup()
    _L0_xattn_in = {k: v for k, v in _L0_xattn_all.items() if k in ('wq_w', 'wq_b', 'wk_w', 'wk_b', 'wv_w', 'wv_b', 'dense_w', 'dense_b')}
    del _L0_xattn_all

    def _L0_ffn_setup():
        import jax, jax.numpy as jnp
        import numpy as np
        B, S, D, E, H, K = (4, 256, 128, 8, 64, 2)
        key = jax.random.key(seed)
        ks = jax.random.split(key, 11)
        sc = 0.02
        return {'x': jax.random.normal(ks[0], (B, S, D), dtype=jnp.float32), 'gate_W': jax.random.normal(ks[1], (D, E), dtype=jnp.float32) * sc, 'W1': jax.random.normal(ks[2], (E, D, H), dtype=jnp.float32) * sc, 'b1': jnp.zeros((E, H), dtype=jnp.float32), 'W2': jax.random.normal(ks[3], (E, H, D), dtype=jnp.float32) * sc, 'b2': jnp.zeros((E, D), dtype=jnp.float32), 'Ws1': jax.random.normal(ks[4], (D, H), dtype=jnp.float32) * sc, 'bs1': jnp.zeros((H,), dtype=jnp.float32), 'Ws2': jax.random.normal(ks[5], (H, D), dtype=jnp.float32) * sc, 'bs2': jnp.zeros((D,), dtype=jnp.float32), 'route_scale': jnp.ones((), dtype=jnp.float32)}
    _L0_ffn_all = _L0_ffn_setup()
    _L0_ffn_in = {k: v for k, v in _L0_ffn_all.items() if k in ('gate_W', 'W1', 'b1', 'W2', 'b2', 'Ws1', 'bs1', 'Ws2', 'bs2', 'route_scale')}
    del _L0_ffn_all
    return {'x': x, 'ctx_1024': ctx_1024, 'g_xattn': g_xattn, 'g_ffn': g_ffn, 'L0_xattn_wq_w': _L0_xattn_in['wq_w'], 'L0_xattn_wq_b': _L0_xattn_in['wq_b'], 'L0_xattn_wk_w': _L0_xattn_in['wk_w'], 'L0_xattn_wk_b': _L0_xattn_in['wk_b'], 'L0_xattn_wv_w': _L0_xattn_in['wv_w'], 'L0_xattn_wv_b': _L0_xattn_in['wv_b'], 'L0_xattn_dense_w': _L0_xattn_in['dense_w'], 'L0_xattn_dense_b': _L0_xattn_in['dense_b'], 'L0_ffn_gate_W': _L0_ffn_in['gate_W'], 'L0_ffn_W1': _L0_ffn_in['W1'], 'L0_ffn_b1': _L0_ffn_in['b1'], 'L0_ffn_W2': _L0_ffn_in['W2'], 'L0_ffn_b2': _L0_ffn_in['b2'], 'L0_ffn_Ws1': _L0_ffn_in['Ws1'], 'L0_ffn_bs1': _L0_ffn_in['bs1'], 'L0_ffn_Ws2': _L0_ffn_in['Ws2'], 'L0_ffn_bs2': _L0_ffn_in['bs2'], 'L0_ffn_route_scale': _L0_ffn_in['route_scale']}

def reference(x, ctx_1024, g_xattn, g_ffn, L0_xattn_wq_w, L0_xattn_wq_b, L0_xattn_wk_w, L0_xattn_wk_b, L0_xattn_wv_w, L0_xattn_wv_b, L0_xattn_dense_w, L0_xattn_dense_b, L0_ffn_gate_W, L0_ffn_W1, L0_ffn_b1, L0_ffn_W2, L0_ffn_b2, L0_ffn_Ws1, L0_ffn_bs1, L0_ffn_Ws2, L0_ffn_bs2, L0_ffn_route_scale):
    import jax
    import jax.numpy as jnp

    def _L0_xattn_ref(v, k, q, wq_w, wq_b, wk_w, wk_b, wv_w, wv_b, dense_w, dense_b):
        import jax, jax.numpy as jnp
        import numpy as np
        D_MODEL = 128
        NUM_HEADS = 16
        DEPTH = D_MODEL // NUM_HEADS

        def _split_heads(x):
            B, S, _ = x.shape
            return x.reshape(B, S, NUM_HEADS, DEPTH).transpose(0, 2, 1, 3)
        B, S, _ = q.shape
        qh = _split_heads(q @ wq_w.T + wq_b)
        kh = _split_heads(k @ wk_w.T + wk_b)
        vh = _split_heads(v @ wv_w.T + wv_b)
        scale = 1.0 / jnp.sqrt(jnp.float32(DEPTH))
        logits = jnp.einsum('bhqd,bhkd->bhqk', qh, kh) * scale
        attn = jax.nn.softmax(logits, axis=-1)
        out = jnp.einsum('bhqk,bhkd->bhqd', attn, vh)
        out = out.transpose(0, 2, 1, 3).reshape(B, S, D_MODEL)
        return out @ dense_w.T + dense_b

    def _L0_ffn_ref(x, gate_W, W1, b1, W2, b2, Ws1, bs1, Ws2, bs2, route_scale):
        import jax, jax.numpy as jnp
        import numpy as np
        B, S, D, E, H, K = (4, 256, 128, 8, 64, 2)
        scores = jax.nn.sigmoid(x @ gate_W) * route_scale
        topk_scores, topk_idx = jax.lax.top_k(scores, K)
        topk_w = topk_scores / topk_scores.sum(-1, keepdims=True)
        onehot = jax.nn.one_hot(topk_idx, E, dtype=x.dtype)
        gate_full = jnp.einsum('bsk,bske->bse', topk_w, onehot)
        h = jax.nn.gelu(jnp.einsum('bsd,edh->bseh', x, W1) + b1, approximate=False)
        y = jnp.einsum('bseh,ehd->bsed', h, W2) + b2
        expert_out = jnp.einsum('bse,bsed->bsd', gate_full, y)
        shared = jax.nn.gelu(x @ Ws1 + bs1, approximate=False) @ Ws2 + bs2
        return expert_out + shared
    x = x + jnp.tanh(g_xattn[0]) * _L0_xattn_ref(ctx_1024, ctx_1024, _layernorm(x, axis=-1), L0_xattn_wq_w, L0_xattn_wq_b, L0_xattn_wk_w, L0_xattn_wk_b, L0_xattn_wv_w, L0_xattn_wv_b, L0_xattn_dense_w, L0_xattn_dense_b)
    x = x + jnp.tanh(g_ffn[0]) * _L0_ffn_ref(_layernorm(x, axis=-1), L0_ffn_gate_W, L0_ffn_W1, L0_ffn_b1, L0_ffn_W2, L0_ffn_b2, L0_ffn_Ws1, L0_ffn_bs1, L0_ffn_Ws2, L0_ffn_bs2, L0_ffn_route_scale)
    return x

_drawn_inputs = setup_inputs


def setup_inputs(seed=0):
    import zlib

    import numpy as np

    out = dict(_drawn_inputs(seed))
    spreads = {'L0_xattn_wq_b': (0.0, 0.499),
     'L0_xattn_wk_b': (0.0, 0.8),
     'L0_xattn_wv_b': (0.0, 0.1),
     'L0_xattn_dense_b': (0.0, 0.1),
     'L0_ffn_b1': (0.0, 0.8),
     'L0_ffn_b2': (0.0, 0.1),
     'L0_ffn_bs1': (0.0, 0.8),
     'L0_ffn_bs2': (0.0, 0.1)}
    factors = {'L0_ffn_W1': 4.911, 'L0_ffn_W2': 4.434, 'L0_ffn_Ws1': 3.432, 'L0_ffn_Ws2': 3.002}
    for name, (base, spread) in spreads.items():
        noise = np.random.default_rng([zlib.crc32(name.encode()), seed]).standard_normal(out[name].shape)
        drawn = base * np.exp(spread * noise) if base else spread * noise
        out[name] = jnp.asarray(drawn.astype(out[name].dtype))
    for name, factor in factors.items():
        out[name] = (out[name] * factor).astype(out[name].dtype)
    return out
```

```python
from contextlib import ExitStack

import numpy as np

import concourse.bass as bass
from concourse import mybir

BATCH, SEQ, D, CTX, HEADS = 16, 256, 128, 1601, 16
DH = D // HEADS
PAIRS = HEADS // 2
QTILES = SEQ // 128
TILES = BATCH * QTILES
CHUNK = 512
CHUNKS = BATCH * SEQ // CHUNK
EXPERTS, HID = 8, 64
GELU_TILES = EXPERTS * HID // 128
EPS = 1e-5
SCALE = float(DH) ** -0.5

KTILES = (CTX + 127) // 128
KEY0 = [min(128 * t, CTX - 128) for t in range(KTILES)]
REPEATED = 128 * (KTILES - 1) - KEY0[-1]
RUN = 401
RUN0 = [400 * i for i in range(4)]
KRUN = [(0, 401), (401, 400), (801, 400), (1201, 400)]

KPART = [0, 1, 2, 0, 1, 0]
QPART = [0, 0, 0, 1, 1, 2]
ROWS = 16 * len(KPART)
MROWS = ROWS + 3

GP = PAIRS // 2
STEPS = 2 * BATCH
UNITS = KTILES * GP
SUNITS = 2 * GP * QTILES * 2
FIRST, LAST = -4, STEPS
LOOP0, PERIOD = 4, 4
TURNS = 5
STB, PB = 3, 8

ALU = mybir.AluOpType
ACT = mybir.ActivationFunctionType
AX = mybir.AxisListType
F32 = mybir.dt.float32
BF16 = mybir.dt.bfloat16


def scored(s):
    return UNITS * min(max(s, 0), STEPS)


def aux_kinds(s):
    b, units = s // 2, []
    if s % 2 == 0 and 0 <= b + 2 < BATCH:
        units += [("K", 0), ("K", 1)]
    if s % 2 == 1 and 0 <= b + 1 < BATCH:
        units += [("V", 0), ("V", 1)]
    if 0 <= s + 1 < STEPS:
        units += [("T", 0)]
    if 0 <= s + 2 < STEPS:
        units += [("S", i) for i in range(SUNITS)]
    if s % 2 == 0 and 0 <= b - 1 < BATCH:
        units += [("D", 0)]
    return units


def aux_before(s):
    return sum(len(aux_kinds(r)) for r in range(FIRST, s))


def aux_until(s, kind):
    kinds = [k for k, _ in aux_kinds(s)]
    return aux_before(s) + len(kinds) - kinds[::-1].index(kind)


class Step:

    def __init__(self, s, turn=None):
        self.s, self.turn = s, turn

    def at(self, count, ds=0):
        first = count(self.s + ds)
        if self.turn is None:
            return first
        grows = count(self.s + ds + PERIOD) - first
        for i in range(TURNS):
            assert count(self.s + ds + PERIOD * i) == first + i * grows
        return self.turn * grows + first if grows else first

    def back(self, ds):
        return Step(self.s + ds, self.turn)


def wait(eng, sem, value):
    if not isinstance(value, int) or value > 0:
        eng.wait_ge(sem, value)


def run_chunks(eng, body):
    body(0)
    with eng.Fori(1, CHUNKS) as c:
        body(c)


def run_steps(eng, body):
    for s in range(FIRST, LOOP0):
        body(Step(s))
    with eng.Fori(0, TURNS) as turn:
        for u in range(PERIOD):
            body(Step(LOOP0 + u, turn))
    for s in range(LOOP0 + PERIOD * TURNS, LAST + 1):
        body(Step(s))


def flamingo_block(nc, x, ctx_t, wq, wk, wv, wd, bq, bk, bv, bd, g_attn, g_ffn,
                   gate_w, w1, ws1, w2, ws2, b1, bs1, b2s, route, ident_in, earlier_in, pick_in, out):
    with ExitStack() as ctx:
        def sb(name, shape, dt=F32):
            return ctx.enter_context(nc.sbuf_tensor(name, shape, dt))

        def sem(name):
            return ctx.enter_context(nc.semaphore(name))

        q_dram = nc.dram_tensor("q_dram", [3, 128, BATCH, 2 * SEQ], BF16, kind="Internal").ap()
        k_dram = nc.dram_tensor("k_dram", [2, 3, 128, CTX], BF16, kind="Internal").ap()
        m_dram = nc.dram_tensor("m_dram", [2, 3, 2 * GP, SEQ], BF16, kind="Internal").ap()
        o_dram = nc.dram_tensor("o_dram", [2, 128, 2 * SEQ], F32, kind="Internal").ap()

        st_ps = [ctx.enter_context(nc.psum_tensor(f"st_ps{i}", [128, 512], F32)) for i in range(STB)]
        o_ps = ctx.enter_context(nc.psum_tensor("o_ps", [128, 512], F32))
        aux_ps = [ctx.enter_context(nc.psum_tensor(f"aux_ps{i}", [128, 2, 512], F32)) for i in range(2)]

        wq_s, wk_s, wv_s, wd_s = (sb(n, [128, 128]) for n in ("wq_s", "wk_s", "wv_s", "wd_s"))
        bq_s, bk_s, gx_s, gf_s, route_s = (sb(n, [128, 1]) for n in ("bq_s", "bk_s", "gx_s", "gf_s", "route_s"))
        one = sb("one", [128, 1])
        tgx, tgf = sb("tgx", [128, 1]), sb("tgf", [128, 1])
        bv_s, bd_s = sb("bv_s", [128, 128]), sb("bd_s", [128, 128])
        ident, earlier = sb("ident", [128, 128]), sb("earlier", [128, EXPERTS, EXPERTS])
        pick = sb("pick", [EXPERTS, GELU_TILES, 128])
        gate_s, w1_s, ws1_s = sb("gate_s", [128, EXPERTS]), sb("w1_s", [128, EXPERTS * HID]), sb("ws1_s", [128, HID])
        w2_s, ws2_s = sb("w2_s", [128, GELU_TILES, 128]), sb("ws2_s", [HID, 128])
        b1_s, bs1_s, b2s_s = sb("b1_s", [128, GELU_TILES]), sb("bs1_s", [HID, 1]), sb("b2s_s", [EXPERTS + 1, 128])
        x_s = sb("x_s", [128, TILES, 128])
        mv, sd, rstd = sb("mv", [128, TILES, 2]), sb("sd", [128, TILES]), sb("rstd", [128, TILES])
        xn = sb("xn", [128, 4, 128])
        xn_t = sb("xn_t", [128, CHUNK])
        q_t = sb("q_t", [128, CHUNK])
        q_parts = sb("q_parts", [128, 3, 2, 2, SEQ], BF16)
        kctx, vctx = sb("kctx", [128, CTX]), sb("vctx", [128, CTX])
        k_t = sb("k_t", [128, CTX])
        stats = k_t[:, 0:6 * TILES].rearrange("p (t c) -> p t c", c=6)
        k_parts = sb("k_parts", [128, 3, CTX], BF16)
        k_op = [sb(f"k_op{i}", [MROWS, GP, CTX], BF16) for i in range(4)]
        q_op = [sb(f"q_op{i}", [MROWS, 2 * GP, SEQ], BF16) for i in range(4)]
        v_op = [sb(f"v_op{i}", [128, KTILES, PAIRS, 32]) for i in range(2)]
        probs = sb("probs", [128, PB, 512])
        run_max = sb("run_max", [128, QTILES * 2 * GP, 2])
        neg_max = sb("neg_max", [128, QTILES, 2 * GP])
        nm_t, nm_rest = sb("nm_t", [2 * GP, SEQ]), sb("nm_rest", [2 * GP, SEQ])
        nm_parts = sb("nm_parts", [2 * GP, 3, SEQ], BF16)
        o_s = [sb(f"o_s{i}", [128, 512]) for i in range(2)]
        num, den, attn = sb("num", [128, SEQ]), sb("den", [128, SEQ]), sb("attn", [128, SEQ])
        logits, score = sb("logits", [128, TILES, EXPERTS]), sb("score", [128, TILES, EXPERTS])
        beats = k_t[:, 0:4 * 64].rearrange("p (t a b) -> p t a b", a=EXPERTS, b=EXPERTS)
        ties = k_t[:, 512:512 + 4 * 64].rearrange("p (t a b) -> p t a b", a=EXPERTS, b=EXPERTS)
        rank, wsum, winv = sb("rank", [128, 4, EXPERTS]), sb("wsum", [128, 4]), sb("winv", [128, 4])
        g_tok = sb("g_tok", [128, 4, EXPERTS])
        g_t = sb("g_t", [EXPERTS + 1, CHUNK])
        hid = probs[:, 0:GELU_TILES, :]
        hid_s = sb("hid_s", [HID, CHUNK])
        hid_g = probs[:, GELU_TILES:2 * GELU_TILES, :]
        y_s = sb("y_s", [128, 4, 128])
        xn_keep = sb("xn_keep", [128, CHUNK])

        const_in, x_in, init = sem("const_in"), sem("x_in"), sem("init")
        tanh_done, xb_done = sem("tanh_done"), sem("xb_done")
        stat_seq, sd_ready, rstd_ready, ve_ready = sem("stat_seq"), sem("sd_ready"), sem("rstd_ready"), sem("ve_ready")
        xn_ready, tr_ready, xnt_ready, proj_ready, qt_ready = (sem(n) for n in
            ("xn_ready", "tr_ready", "xnt_ready", "proj_ready", "qt_ready"))
        q_chain, q_written = sem("q_chain"), sem("q_written")
        kctx_in, vctx_in = sem("kctx_in"), sem("vctx_in")
        op_in = [sem(f"op_in{i}") for i in range(4)]
        m_written, m_in = sem("m_written"), [sem(f"m_in{i}") for i in range(2)]
        k_written = sem("k_written")
        st_ready, exp_done, p_used = sem("st_ready"), sem("exp_done"), sem("p_used")
        aux_ready, aux_free = sem("aux_ready"), sem("aux_free")
        v_ready, nm_ready, m_chain, k_chain = sem("v_ready"), sem("nm_ready"), sem("m_chain"), sem("k_chain")
        o_copied, o_written, o_in = sem("o_copied"), sem("o_written"), [sem(f"o_in{i}") for i in range(2)]
        norm_seq = sem("norm_seq")
        f_dve, f_pe, f_act = sem("f_dve"), sem("f_pe"), sem("f_act")
        f_dve_a, sig_ready, gate_seq, gt_ready = (sem(n) for n in ("f_dve_a", "sig_ready", "gate_seq", "gt_ready"))
        out_done = sem("out_done")

        consts = [(wq_s, wq), (wk_s, wk), (wv_s, wv), (wd_s, wd), (bq_s, bq), (bk_s, bk), (bv_s, bv), (bd_s, bd),
                  (gx_s, g_attn), (gf_s, g_ffn), (route_s, route), (ident, ident_in), (earlier, earlier_in),
                  (pick, pick_in), (gate_s, gate_w), (w1_s, w1), (ws1_s, ws1), (w2_s, w2), (ws2_s, ws2),
                  (b1_s, b1), (bs1_s, bs1), (b2s_s, b2s)]
        ALL_CONSTS = 16 * len(consts)
        STATS = TILES + 1
        FD = 2 + GELU_TILES + 1
        FP = 2 + GELU_TILES + 1 + GELU_TILES + 1
        INIT0, INIT = 9, 11

        block = ctx.enter_context(nc.Block())

        @block.sync
        def _(sp):
            for t in range(CHUNKS):
                sp.dma_start(x_s[:, 4 * t:4 * t + 4, :], x[:, 4 * t:4 * t + 4, :]).then_inc(x_in, 16)
            for dst, src in consts:
                sp.dma_start(dst[tuple([slice(None)] * len(src.shape))], src).then_inc(const_in, 16)
            sp.dma_start(kctx[:, :], ctx_t[0]).then_inc(kctx_in, 16)
            sp.dma_start(vctx[:, :], ctx_t[0]).then_inc(vctx_in, 16)

            registers = [ctx.enter_context(sp.register(f"sp_value{i}")) for i in range(16)]

            def held(v, i, top=None):
                if isinstance(v, int):
                    return v
                sp.reg_mov(registers[i], v)
                return registers[i] if top is None else sp.snap(registers[i], min_val=0, max_val=top)

            def q_out(c):
                split, first = 8 * c + 8, 2 * c
                split, first = held(split, 0), held(first, 1, BATCH - 2)
                sp.wait_ge(q_chain, split)
                for part in range(3):
                    sp.dma_start(q_dram[part, :, bass.ds(first, 2), :],
                                 q_parts[:, part].rearrange("p b a q -> p b (a q)")).then_inc(q_written, 16)
            run_chunks(sp, q_out)
            sp.wait_ge(q_written, 48 * CHUNKS)
            sp.wait_ge(init, INIT)

            def step(st):
                s = st.s
                b = s // 2
                used = []

                def value(count, ds=0, top=None):
                    used.append(0)
                    return held(st.at(count, ds), len(used) - 1, top)

                def at(i):
                    return i if isinstance(i, int) else bass.ds(i, 1)

                load_op = 0 <= s + 3 < STEPS
                store_o = 0 <= s - 1 < STEPS
                load_kctx = s % 2 == 0 and 0 <= b + 2 and b + 3 < BATCH
                load_vctx = s % 2 == 1 and 0 <= b + 1 and b + 2 < BATCH
                move_max = 0 <= s + 1 < STEPS
                store_k = s % 2 == 0 and 0 <= b + 2 < BATCH
                if load_op:
                    batch = value(lambda r: r // 2, 3, BATCH - 1)
                    scores_done = value(scored)
                    k_stored = value(lambda r: 48 * (r // 2 + 1), 3)
                if store_o:
                    o_ready = value(lambda r: r)
                    o_read = value(lambda r: 64 * ((r - 1) // 2))
                    o_stored = value(lambda r: 16 * r)
                    normalised = value(lambda r: 2 * ((r - 1) // 2)) if s % 2 == 1 else 0
                if load_kctx:
                    k_projected, k_batch = value(lambda r: aux_until(r, "K")), value(lambda r: r // 2, 6, BATCH - 1)
                if load_vctx:
                    v_projected, v_batch = value(lambda r: aux_until(r, "V")), value(lambda r: r // 2, 4, BATCH - 1)
                if move_max:
                    max_split, m_read = value(lambda r: 4 * (r + 1), 1), value(lambda r: 16 * (r // 2), 1)
                    m_stored = value(lambda r: 16 * (r + 1), 1)
                if store_k:
                    k_split = value(lambda r: 4 * (r // 2 + 1), 4)
                    loaded = [value(lambda r: 144 * ((r + d) // 4 + 1)) if s >= 0 else 0 for d in (0, 1)]

                if load_op:
                    buf, g = (s + 3) % 4, (s + 3) % 2
                    wait(sp, st_ready, scores_done)
                    wait(sp, k_written, k_stored)
                    kd = k_dram[((s + 3) // 2) % 2].rearrange("n (a p) c -> (n a) p c", p=PAIRS)
                    qd = q_dram.rearrange("n (a p) b q -> n a p b q", p=PAIRS)
                    pairs = slice(GP * g, GP * g + GP)
                    for r0, r1 in ((0, 48), (48, 80), (80, 96)):
                        sp.dma_start(k_op[buf][r0:r1, :, :], kd[0:r1 - r0, pairs, :]).then_inc(op_in[buf], 16)
                    for r, part in enumerate(QPART):
                        src = qd[part, :, pairs, at(batch), :]
                        if not isinstance(batch, int):
                            src = src.rearrange("a p b q -> a p (b q)")
                        sp.dma_start(q_op[buf][16 * r:16 * r + 16, :, :].rearrange("r (p a) q -> r p (a q)", a=2),
                                     src).then_inc(op_in[buf], 16)
                if store_o:
                    h = (s - 1) % 2
                    wait(sp, o_copied, o_ready)
                    wait(sp, o_in[h], o_read)
                    sp.dma_start(o_dram[h], o_s[h][:, :]).then_inc(o_written, 16)
                    sp.wait_ge(o_written, o_stored)
                    wait(sp, norm_seq, normalised)
                    od = o_dram[h].rearrange("(j r) q -> j r q", r=32)
                    for side in range(2):
                        to = slice(64 * side + 32 * h, 64 * side + 32 * h + 32)
                        cols = slice(SEQ * side, SEQ * side + SEQ)
                        sp.dma_start(num[to, :], od[:, 8 * side:8 * side + 8, cols]).then_inc(o_in[h], 16)
                        sp.dma_start(den[to, :], od[:, 16:24, cols]).then_inc(o_in[h], 16)
                if load_kctx or load_vctx:
                    sp.wait_ge(aux_ready, k_projected if load_kctx else v_projected)
                    dst, i, arrived = (kctx, k_batch, kctx_in) if load_kctx else (vctx, v_batch, vctx_in)
                    src = ctx_t[at(i)]
                    if not isinstance(i, int):
                        src = src.rearrange("o p c -> (o p) c")
                    sp.dma_start(dst[:, :], src).then_inc(arrived, 16)
                if move_max:
                    h = (s + 1) % 2
                    sp.wait_ge(m_chain, max_split)
                    wait(sp, m_in[h], m_read)
                    sp.dma_start(m_dram[h].rearrange("n h q -> h n q"), nm_parts[:, :, :]).then_inc(m_written, 16)
                    sp.wait_ge(m_written, m_stored)
                    sp.dma_start(q_op[(s + 1) % 4][ROWS:MROWS, :, :], m_dram[h]).then_inc(m_in[h], 16)
                if store_k:
                    sp.wait_ge(k_chain, k_split)
                    for d in (0, 1):
                        wait(sp, op_in[(s + d) % 4], loaded[d])
                    for part in range(3):
                        sp.dma_start(k_dram[(b + 2) % 2, part], k_parts[:, part, :]).then_inc(k_written, 16)
            run_steps(sp, step)

            with sp.Fori(0, CHUNKS) as c:
                ready, first = held(c * FD + FD, 0), held(c * 4, 1, TILES - 4)
                sp.wait_ge(f_dve, ready)
                sp.dma_start(out[:, bass.ds(first, 4), :], y_s[:, :, :]).then_inc(out_done, 16)
            sp.wait_ge(out_done, 16 * CHUNKS)

        @block.gpsimd
        def _(pool):
            for i in range(4):
                pool.memset(k_op[i][ROWS:MROWS, :, :], 1.0).then_inc(init, 1)
            pool.wait_ge(init, 4)
            pool.memset(q_parts[:, :, :, :, :], 0.0).then_inc(init, 1)
            for i in range(2):
                pool.memset(v_op[i][:, :, :, 16:32], 1.0).then_inc(init, 1)
            pool.memset(g_t[:, :], 1.0).then_inc(init, 1)
            pool.memset(one[:, :], 1.0).then_inc(init, 1)
            pool.wait_ge(init, INIT0)
            for i in range(2):
                pool.memset(v_op[i][0:REPEATED, KTILES - 1, :, :], 0.0).then_inc(init, 1)

            def ones(like, rows_of=slice(0, 128)):
                factor = one[rows_of, :]
                while len(factor.shape) < len(like.shape):
                    factor = factor.unsqueeze(1)
                return factor.broadcast_to(list(like.shape))

            def q_split(c):
                pool.wait_ge(qt_ready, c + 1)
                if not isinstance(c, int) or c > 0:
                    pool.wait_ge(q_written, c * 48)
                sides = [(slice(0, 64), 0), (slice(64, 128), 1)]
                qv = q_t[:, :].rearrange("p (b q) -> p b q", b=2)
                n = 0
                for part in range(3):
                    for rows, side in sides:
                        piece = q_parts[rows, part, :, side, :]
                        if part < 2:
                            pool.tensor_tensor(piece, qv[rows], ones(qv[rows], rows), ALU.mult).then_inc(q_chain, 1)
                            n += 1
                    if part < 2:
                        pool.wait_ge(q_chain, c * 8 + n)
                    for rows, side in sides:
                        if part == 0:
                            pool.tensor_tensor(qv[rows], qv[rows], q_parts[rows, 0, :, side, :],
                                               ALU.subtract).then_inc(q_chain, 1)
                            n += 1
                        if part == 1:
                            pool.tensor_tensor(q_parts[rows, 2, :, side, :], qv[rows], q_parts[rows, 1, :, side, :],
                                               ALU.subtract).then_inc(q_chain, 1)
                            n += 1
                    if part == 0:
                        pool.wait_ge(q_chain, c * 8 + n)
            run_chunks(pool, q_split)
            pool.wait_ge(q_chain, 8 * CHUNKS)

            def split3(chain, done, whole, parts, rest):
                pool.tensor_tensor(parts[0], whole, ones(whole, slice(0, whole.shape[0])), ALU.mult).then_inc(chain, 1)
                pool.wait_ge(chain, done + 1)
                pool.tensor_tensor(rest, whole, parts[0], ALU.subtract).then_inc(chain, 1)
                pool.wait_ge(chain, done + 2)
                pool.tensor_tensor(parts[1], rest, ones(rest, slice(0, rest.shape[0])), ALU.mult).then_inc(chain, 1)
                pool.wait_ge(chain, done + 3)
                pool.tensor_tensor(parts[2], rest, parts[1], ALU.subtract).then_inc(chain, 1)

            def step(st):
                s = st.s
                if 0 <= s + 1 < STEPS:
                    pool.wait_ge(aux_free, st.at(lambda r: aux_until(r, "T")))
                    wait(pool, m_written, st.at(lambda r: 16 * r, 1))
                    split3(m_chain, st.at(lambda r: 4 * r, 1), nm_t[:, :],
                           [nm_parts[:, i, :] for i in range(3)], nm_rest[:, :])
                if s % 2 == 0 and 0 <= s // 2 + 2 < BATCH:
                    pool.wait_ge(aux_free, st.at(lambda r: aux_until(r, "K")))
                    wait(pool, k_written, st.at(lambda r: 48 * (r // 2), 4))
                    split3(k_chain, st.at(lambda r: 4 * (r // 2), 4), k_t[:, :],
                           [k_parts[:, i, :] for i in range(3)], k_t[:, :])
            run_steps(pool, step)

        @block.scalar
        def _(act):
            act.wait_ge(const_in, ALL_CONSTS)
            act.activation(tgx[:, :], gx_s[:, :], ACT.Tanh).then_inc(tanh_done, 1)
            act.activation(tgf[:, :], gf_s[:, :], ACT.Tanh).then_inc(tanh_done, 1)
            act.wait_ge(ve_ready, 1)
            act.activation(sd[:, :], sd[:, :], ACT.Sqrt).then_inc(sd_ready, 1)

            def step(st):
                s = st.s
                if not 0 <= s < STEPS:
                    return
                for i in range(UNITS):
                    act.wait_ge(st_ready, st.at(lambda r: scored(r) + i + 1))
                    if scored(s) + i >= PB:
                        act.wait_ge(p_used, st.at(lambda r: scored(r) + i + 1 - PB))
                    act.activation(probs[:, (scored(s) + i) % PB, :], st_ps[(i + s % 4) % STB][:, :], ACT.Exp,
                                   scale=SCALE).then_inc(exp_done, 1)
            run_steps(act, step)

            act.wait_ge(p_used, scored(STEPS))
            act.wait_ge(ve_ready, 2)
            act.activation(sd[:, :], sd[:, :], ACT.Sqrt).then_inc(sd_ready, 1)
            act.wait_ge(f_dve_a, CHUNKS)
            act.activation(score[:, :, :], logits[:, :, :], ACT.Exp, scale=-1.0).then_inc(sig_ready, 1)
            with act.Fori(0, CHUNKS) as c:
                for m in range(GELU_TILES + 1):
                    act.wait_ge(f_pe, c * FP + (3 + m))
                    ps = st_ps[m] if m < 3 else aux_ps[1][:, m - 3, :]
                    if m < GELU_TILES:
                        act.activation(hid[:, m, :], ps[:, :] if m < 3 else ps, ACT.Gelu,
                                       bias=b1_s[:, m:m + 1]).then_inc(f_act, 1)
                    else:
                        act.activation(hid_s[:, :], aux_ps[1][0:HID, 1, :], ACT.Gelu,
                                       bias=bs1_s[:, 0:1]).then_inc(f_act, 1)

        @block.tensor
        def _(pe):
            pe.wait_ge(const_in, ALL_CONSTS)

            def transpose4(src, bank, signal):
                for t in range(4):
                    last = pe.transpose(bank[:, 128 * t:128 * t + 128], src[:, t, :], ident[:, :])
                last.then_inc(signal, 1)

            with pe.Fori(0, CHUNKS) as c:
                pe.wait_ge(xn_ready, c * 4 + 4)
                transpose4(xn, aux_ps[0][:, 0, :], tr_ready)
                pe.wait_ge(xnt_ready, c + 1)
                pe.matmul(aux_ps[1][:, 0, :], wq_s[:, :], xn_t[:, :], start=True, stop=True).then_inc(proj_ready, 1)
            pe.wait_ge(qt_ready, CHUNKS)
            pe.wait_ge(init, INIT)

            def aux_unit(st, n, kind, i):
                s = st.s
                number = st.at(lambda r: aux_before(r) + n)
                slot = aux_ps[(aux_before(s) + n) % 2]
                if aux_before(s) + n >= 2:
                    pe.wait_ge(aux_free, number - 1)
                if kind == "K":
                    pe.wait_ge(kctx_in, st.at(lambda r: 16 * (r // 2 + 1), 4))
                    for j in range(2):
                        k0, n_keys = KRUN[2 * i + j]
                        last = pe.matmul(slot[:, j, 0:n_keys], wk_s[:, :], kctx[:, k0:k0 + n_keys],
                                         start=True, stop=True)
                elif kind == "V":
                    pe.wait_ge(vctx_in, st.at(lambda r: 16 * (r // 2 + 1), 2))
                    for t in range(8 * i, min(8 * i + 8, KTILES)):
                        last = pe.matmul(slot[:, t % 8 // 4, 128 * (t % 4):128 * (t % 4) + 128],
                                         vctx[:, KEY0[t]:KEY0[t] + 128], wv_s[:, :], start=True, stop=True)
                elif kind == "T":
                    pe.wait_ge(nm_ready, st.at(lambda r: r + 1, 1))
                    for t in range(QTILES):
                        last = pe.transpose(slot[0:2 * GP, 0, 128 * t:128 * t + 128], neg_max[:, t, :], ident[:, :])
                elif kind == "S":
                    buf = (s + 2) % 4
                    if i == 0:
                        pe.wait_ge(op_in[buf], st.at(lambda r: 144 * (r // 4 + 1), 2))
                    h, t, half = i // 4, i // 2 % 2, i % 2
                    for j in range(2):
                        k0 = RUN0[2 * half + j]
                        last = pe.matmul(slot[:, j, 0:RUN], q_op[buf][0:ROWS, h, 128 * t:128 * t + 128],
                                         k_op[buf][0:ROWS, h // 2, k0:k0 + RUN], start=True, stop=True)
                else:
                    pe.wait_ge(norm_seq, st.at(lambda r: 2 * (r // 2)))
                    for t in range(QTILES):
                        last = pe.matmul(slot[:, 0, 128 * t:128 * t + 128], attn[:, 128 * t:128 * t + 128],
                                         wd_s[:, :], start=True, stop=True)
                last.then_inc(aux_ready, 1)

            def scores(st, i):
                s = st.s
                buf = s % 4
                if i == 0:
                    pe.wait_ge(m_in[s % 2], st.at(lambda r: 16 * (r // 2 + 1)))
                behind = 0 if i == 0 and s % 4 == 0 else i - STB + 1
                if scored(s) + behind > 0:
                    pe.wait_ge(exp_done, st.at(lambda r: scored(r) + behind))
                t, j = i // GP, i % GP
                pe.matmul(st_ps[(i + s % 4) % STB][:, :], k_op[buf][:, j, KEY0[t]:KEY0[t] + 128],
                          q_op[buf][:, 2 * j:2 * j + 2, :], start=True, stop=True).then_inc(st_ready, 1)

            def values(st, i):
                s = st.s
                t, j = i // GP, i % GP
                pe.wait_ge(exp_done, st.at(lambda r: scored(r) + i + 1))
                if i == 0:
                    pe.wait_ge(v_ready, st.at(lambda r: r // 2 + 1))
                    wait(pe, o_copied, st.at(lambda r: r))
                pair = GP * (s % 2) + j
                pe.matmul(o_ps[32 * j:32 * j + 32, :], v_op[s // 2 % 2][:, t, pair, :],
                          probs[:, (scored(s) + i) % PB, :], start=(t == 0), stop=(t == KTILES - 1)).then_inc(p_used, 1)

            def step(st):
                s = st.s
                units = list(enumerate(aux_kinds(s)))
                for quad in range(KTILES):
                    for j in range(GP):
                        if 0 <= s < STEPS:
                            scores(st, GP * quad + j)
                        end = quad == KTILES - 1 and j == 2
                        if j < 3 and units and (end or units[0][1][0] != "D"):
                            n, (kind, i) = units.pop(0)
                            aux_unit(st, n, kind, i)
                    for j in range(GP):
                        if quad == 0 and 0 <= s - 1 < STEPS:
                            values(st.back(-1), UNITS - GP + j)
                        if quad > 0 and 0 <= s < STEPS:
                            values(st, GP * (quad - 1) + j)
                assert not units
            run_steps(pe, step)

            with pe.Fori(0, CHUNKS) as c:
                pe.wait_ge(xn_ready, c * 4 + (4 + 4 * CHUNKS))
                transpose4(xn, aux_ps[0][:, 0, :], tr_ready)
                pe.wait_ge(xnt_ready, c + (1 + CHUNKS))
                for t in range(4):
                    last = pe.matmul(aux_ps[1][:, 0, 8 * t:8 * t + 8], xn_t[:, 128 * t:128 * t + 128], gate_s[:, :],
                                     start=True, stop=True)
                last.then_inc(proj_ready, 1)
            pe.wait_ge(f_dve_a, CHUNKS)
            with pe.Fori(0, CHUNKS) as c:
                pe.wait_ge(xn_ready, c * 4 + (4 + 8 * CHUNKS))
                transpose4(xn, aux_ps[0][:, 0, :], f_pe)
                pe.wait_ge(gt_ready, c + 1)
                for t in range(4):
                    last = pe.transpose(aux_ps[0][0:EXPERTS, 1, 128 * t:128 * t + 128], g_tok[:, t, :], ident[:, :])
                last.then_inc(f_pe, 1)
                pe.wait_ge(f_dve, c * FD + 1)
                for m in range(GELU_TILES):
                    ps = st_ps[m][:, :] if m < 3 else aux_ps[1][:, 0, :]
                    pe.matmul(ps, w1_s[:, 128 * m:128 * m + 128], xn_keep[:, :], start=True, stop=True).then_inc(f_pe, 1)
                pe.matmul(aux_ps[1][0:HID, 1, :], ws1_s[:, :], xn_keep[:, :], start=True, stop=True).then_inc(f_pe, 1)
                pe.wait_ge(f_dve, c * FD + 2)
                for m in range(GELU_TILES):
                    if m > 0:
                        pe.wait_ge(f_act, c * 5 + m)
                    ps = aux_ps[0][:, 0, :] if m == 0 else st_ps[m - 1][:, :]
                    pe.matmul(ps, pick[:, m, :], g_t[0:EXPERTS, :], start=True, stop=True).then_inc(f_pe, 1)
                pe.wait_ge(f_act, c * 5 + 5)
                pe.wait_ge(f_dve, c * FD + 6)
                for t in range(4):
                    tok = slice(128 * t, 128 * t + 128)
                    for m in range(GELU_TILES):
                        pe.matmul(o_ps[:, tok], hid_g[:, m, tok], w2_s[:, m, :], start=(m == 0), stop=False)
                    pe.matmul(o_ps[:, tok], hid_s[:, tok], ws2_s[:, :], start=False, stop=False)
                    last = pe.matmul(o_ps[:, tok], g_t[:, tok], b2s_s[:, :], start=False, stop=True)
                last.then_inc(f_pe, 1)
                pe.wait_ge(f_dve, c * FD + 7)

        @block.vector
        def _(dve):
            def statistics(base, ve):
                for t in range(TILES):
                    dve.bn_stats(stats[:, t, :], x_s[:, t, :]).then_inc(stat_seq, 1)
                for t in range(TILES):
                    dve.wait_ge(stat_seq, base + t + 1)
                    last = dve.bn_aggr(mv[:, t, :], stats[:, t, :])
                last.then_inc(stat_seq, 1)
                dve.wait_ge(stat_seq, base + STATS)
                dve.tensor_scalar(sd[:, :], mv[:, :, 1], EPS, None, ALU.add).then_inc(ve_ready, 1)
                dve.wait_ge(sd_ready, ve)
                dve.reciprocal(rstd[:, :], sd[:, :]).then_inc(rstd_ready, 1)
                dve.wait_ge(rstd_ready, ve)

            def normalise(c):
                for t in range(4):
                    tile = bass.ds(c * 4 + t, 1)
                    dve.tensor_scalar(xn[:, t, :], x_s[:, tile, :].rearrange("p o d -> p (o d)"),
                                      mv[:, tile, 0:1].rearrange("p o d -> p (o d)"), rstd[:, tile],
                                      ALU.subtract, ALU.mult).then_inc(xn_ready, 1)

            dve.wait_ge(x_in, 16 * CHUNKS)
            dve.wait_ge(const_in, ALL_CONSTS)
            statistics(0, 1)
            def project_q(c):
                normalise(c)
                dve.wait_ge(tr_ready, c + 1)
                dve.tensor_copy(xn_t[:, :], aux_ps[0][:, 0, :]).then_inc(xnt_ready, 1)
                dve.wait_ge(proj_ready, c + 1)
                if not isinstance(c, int):
                    dve.wait_ge(q_chain, c * 8)
                dve.tensor_scalar(q_t[:, :], aux_ps[1][:, 0, :], bq_s[:, 0:1], None, ALU.add).then_inc(qt_ready, 1)
            run_chunks(dve, project_q)
            dve.wait_ge(tanh_done, 2)
            dve.tensor_scalar(bd_s[:, :], bd_s[:, :], tgx[:, 0:1], None, ALU.mult).then_inc(xb_done, 1)
            dve.wait_ge(xb_done, 1)
            dve.tensor_tensor(x_s[:, :, :], x_s[:, :, :], bd_s[:, :].unsqueeze(1).broadcast_to([128, TILES, 128]),
                              ALU.add).then_inc(xb_done, 1)
            dve.wait_ge(xb_done, 2)
            dve.wait_ge(init, INIT)

            def aux_unit(st, n, kind, i):
                s = st.s
                slot = aux_ps[(aux_before(s) + n) % 2]
                done = st.at(lambda r: aux_before(r) + n + 1)
                dve.wait_ge(aux_ready, done)
                if kind == "K":
                    if i == 0:
                        wait(dve, k_chain, st.at(lambda r: 4 * (r // 2), 4))
                    for j in range(2):
                        k0, n_keys = KRUN[2 * i + j]
                        last = dve.tensor_scalar(k_t[:, k0:k0 + n_keys], slot[:, j, 0:n_keys], bk_s[:, 0:1], None,
                                                 ALU.add)
                    last.then_inc(aux_free, 1)
                elif kind == "V":
                    v = v_op[(s // 2 + 1) % 2]
                    if i == 0:
                        wait(dve, p_used, st.at(scored, -1))
                    for j in range(2):
                        t0 = 8 * i + 4 * j
                        nt = min(4, KTILES - t0)
                        src = slot[:, j, 0:128 * nt].rearrange("p (t m c) -> p t m c", t=nt, c=16)
                        bias = bv_s[:, :].rearrange("p (m c) -> p m c", c=16).unsqueeze(1)\
                            .broadcast_to([128, nt, PAIRS, 16])
                        last = dve.tensor_tensor(v[:, t0:t0 + nt, :, 0:16], src, bias, ALU.add)
                    last.then_inc(aux_free, 1)
                    if i == 1:
                        dve.wait_ge(aux_free, done)
                        dve.memset(v[0:REPEATED, KTILES - 1, :, 0:16], 0.0).then_inc(v_ready, 1)
                elif kind == "T":
                    wait(dve, m_chain, st.at(lambda r: 4 * r, 1))
                    dve.tensor_copy(nm_t[:, :], slot[0:2 * GP, 0, 0:SEQ]).then_inc(aux_free, 1)
                elif kind == "S":
                    if i == 0:
                        wait(dve, nm_ready, st.at(lambda r: r, 2))
                    h, t, half = i // 4, i // 2 % 2, i % 2
                    dve.tensor_reduce(run_max[:, 2 * GP * t + h, half:half + 1], slot[:, :, 0:RUN], AX.XY,
                                      ALU.max).then_inc(aux_free, 1)
                    if i == SUNITS - 1:
                        dve.wait_ge(aux_free, done)
                        dve.tensor_reduce(neg_max[:, :, :].rearrange("p t h -> p (t h)"), run_max[:, :, :], AX.X,
                                          ALU.max, negate=True).then_inc(nm_ready, 1)
                else:
                    tiles = st.at(lambda r: r - 2)
                    tiles = bass.ds(tiles, 2) if not isinstance(tiles, int) else slice(tiles, tiles + 2)
                    dve.scalar_tensor_tensor(out=x_s[:, tiles, :].rearrange("p t d -> p (t d)"),
                                             in0=slot[:, 0, 0:2 * 128], scalar=tgx[:, 0:1],
                                             in1=x_s[:, tiles, :].rearrange("p t d -> p (t d)"),
                                             op0=ALU.mult, op1=ALU.add).then_inc(aux_free, 1)

            def step(st):
                s = st.s
                units = aux_kinds(s)
                last = len(units) - (("D", 0) in units)
                marks = min(3, last), min(24, last)
                for n in range(len(units) + 1):
                    if n == marks[0] and 0 <= s - 1 < STEPS:
                        dve.wait_ge(p_used, st.at(scored))
                        wait(dve, o_written, st.at(lambda r: 16 * (r - 2)) if s > 2 else 0)
                        dve.tensor_copy(o_s[(s - 1) % 2][:, :], o_ps[:, :]).then_inc(o_copied, 1)
                    if n == marks[1] and s % 2 == 0 and 0 <= s // 2 - 1 < BATCH:
                        for h in range(2):
                            dve.wait_ge(o_in[h], st.at(lambda r: 64 * (r // 2)))
                        dve.reciprocal(den[:, :], den[:, :]).then_inc(norm_seq, 1)
                        dve.wait_ge(norm_seq, st.at(lambda r: 2 * (r // 2) - 1))
                        dve.tensor_tensor(attn[:, :], num[:, :], den[:, :], ALU.mult).then_inc(norm_seq, 1)
                    if n < len(units):
                        aux_unit(st, n, *units[n])
            run_steps(dve, step)
            dve.wait_ge(aux_free, aux_before(LAST + 1))
            dve.wait_ge(k_chain, 4 * BATCH)

            statistics(STATS, 2)
            with dve.Fori(0, CHUNKS) as c:
                normalise(c)
                dve.wait_ge(tr_ready, c + (1 + CHUNKS))
                dve.tensor_copy(xn_t[:, :], aux_ps[0][:, 0, :]).then_inc(xnt_ready, 1)
                dve.wait_ge(proj_ready, c + (1 + CHUNKS))
                dve.tensor_copy(logits[:, bass.ds(c * 4, 4), :],
                                aux_ps[1][:, 0, 0:32].rearrange("p (t e) -> p t e", t=4)).then_inc(f_dve_a, 1)
            dve.wait_ge(sig_ready, 1)
            chain = [0]

            def link(ins):
                chain[0] += 1
                ins.then_inc(gate_seq, 1)
                dve.wait_ge(gate_seq, chain[0])
            link(dve.tensor_scalar(score[:, :, :], score[:, :, :], 1.0, None, ALU.add))
            link(dve.reciprocal(score[:, :, :], score[:, :, :]))
            link(dve.tensor_scalar(score[:, :, :], score[:, :, :], route_s[:, 0:1], None, ALU.mult))
            LINKS, PER = 3, 8

            def chunk_gates(c):
                count = [0]

                def link(ins):
                    count[0] += 1
                    ins.then_inc(gate_seq, 1)
                    dve.wait_ge(gate_seq, c * PER + (LINKS + count[0]))
                sc = score[:, bass.ds(c * 4, 4), :]
                other = sc.unsqueeze(2).broadcast_to([128, 4, EXPERTS, EXPERTS])
                own = sc.unsqueeze(3).broadcast_to([128, 4, EXPERTS, EXPERTS])
                link(dve.tensor_tensor(beats, other, own, ALU.is_gt))
                link(dve.tensor_tensor(ties, other, own, ALU.is_equal))
                link(dve.tensor_tensor(ties, ties, earlier[:, :, :].unsqueeze(1)
                                       .broadcast_to([128, 4, EXPERTS, EXPERTS]), ALU.mult))
                link(dve.tensor_tensor(beats, beats, ties, ALU.add))
                link(dve.tensor_reduce(rank[:, :, :], beats, AX.X, ALU.add))
                link(dve.scalar_tensor_tensor(out=rank[:, :, :], in0=rank[:, :, :], scalar=1.5, in1=sc,
                                              op0=ALU.is_lt, op1=ALU.mult))
                link(dve.tensor_reduce(wsum[:, :], rank[:, :, :], AX.X, ALU.add))
                link(dve.reciprocal(winv[:, :], wsum[:, :]))
                dve.tensor_tensor(g_tok[:, :, :], rank[:, :, :], winv[:, :].unsqueeze(2)
                                  .broadcast_to([128, 4, EXPERTS]), ALU.mult).then_inc(gt_ready, 1)

            def experts(c):
                normalise(c)
                chunk_gates(c)
                dve.wait_ge(f_pe, c * FP + 1)
                dve.tensor_copy(xn_keep[:, :], aux_ps[0][:, 0, :]).then_inc(f_dve, 1)
                dve.wait_ge(f_pe, c * FP + 2)
                dve.tensor_copy(g_t[0:EXPERTS, :], aux_ps[0][0:EXPERTS, 1, :]).then_inc(f_dve, 1)
                for m in range(GELU_TILES):
                    dve.wait_ge(f_pe, c * FP + (8 + m))
                    dve.wait_ge(f_act, c * 5 + (m + 1))
                    ps = aux_ps[0][:, 0, :] if m == 0 else st_ps[m - 1][:, :]
                    dve.tensor_tensor(hid_g[:, m, :], hid[:, m, :], ps, ALU.mult).then_inc(f_dve, 1)
                dve.wait_ge(f_pe, c * FP + 12)
                if not isinstance(c, int):
                    dve.wait_ge(out_done, c * 16)
                tiles = bass.ds(c * 4, 4)
                dve.scalar_tensor_tensor(out=y_s[:, :, :].rearrange("p t d -> p (t d)"), in0=o_ps[:, :],
                                         scalar=tgf[:, 0:1], in1=x_s[:, tiles, :].rearrange("p t d -> p (t d)"),
                                         op0=ALU.mult, op1=ALU.add).then_inc(f_dve, 1)
            run_chunks(dve, experts)


def kernel(**inputs):
    import concourse.bacc as bacc
    from concourse.bass_utils import run_bass_kernel_spmd

    a = {n: np.asarray(v) for n, v in inputs.items()}

    def column(v):
        return v.reshape(-1, 1)

    def rows(v):
        return np.broadcast_to(v.reshape(1, -1), (128, v.size))

    sdp = np.arange(D).reshape(PAIRS, 2 * DH).T.reshape(-1)
    spd = np.arange(D).reshape(PAIRS, 2, DH).transpose(1, 0, 2).reshape(-1)
    earlier = np.tril(np.ones((EXPERTS, EXPERTS), np.float32), -1)
    pick = np.zeros((EXPERTS, GELU_TILES, 128), np.float32)
    for e in range(EXPERTS):
        pick[e, e // 2, HID * (e % 2):HID * (e % 2) + HID] = 1.0
    arrays = {
        "x": a["x"].reshape(TILES, 128, D).transpose(1, 0, 2),
        "ctx_t": a["ctx_1024"].transpose(0, 2, 1),
        "wq": a["L0_xattn_wq_w"][sdp].T, "wk": a["L0_xattn_wk_w"][sdp].T, "wv": a["L0_xattn_wv_w"].T,
        "wd": a["L0_xattn_dense_w"].T[spd],
        "bq": column(a["L0_xattn_wq_b"][sdp]), "bk": column(a["L0_xattn_wk_b"][sdp]),
        "bv": rows(a["L0_xattn_wv_b"]), "bd": rows(a["L0_xattn_dense_b"]),
        "g_attn": rows(a["g_xattn"]), "g_ffn": rows(a["g_ffn"]),
        "gate_w": a["L0_ffn_gate_W"], "w1": a["L0_ffn_W1"].transpose(1, 0, 2).reshape(D, EXPERTS * HID),
        "ws1": a["L0_ffn_Ws1"],
        "w2": a["L0_ffn_W2"].reshape(GELU_TILES, 128, D).transpose(1, 0, 2), "ws2": a["L0_ffn_Ws2"],
        "b1": a["L0_ffn_b1"].reshape(GELU_TILES, 128).T, "bs1": column(a["L0_ffn_bs1"]),
        "b2s": np.concatenate([a["L0_ffn_b2"], a["L0_ffn_bs2"].reshape(1, D)]),
        "route": rows(a["L0_ffn_route_scale"]),
        "ident_in": np.eye(128, dtype=np.float32),
        "earlier_in": np.broadcast_to(earlier, (128, EXPERTS, EXPERTS)),
        "pick_in": pick,
    }
    arrays = {n: np.ascontiguousarray(v) for n, v in arrays.items()}
    nc = bacc.Bacc("TRN2", target_bir_lowering=False, num_devices=1)
    args = [nc.dram_tensor(n, v.shape, mybir.dt.from_np(v.dtype), kind="ExternalInput").ap()
            for n, v in arrays.items()]
    out = nc.dram_tensor("out", (128, TILES, D), F32, kind="ExternalOutput").ap()
    flamingo_block(nc, *args, out)
    r = run_bass_kernel_spmd(nc, [arrays], core_ids=[0])
    y = r.results[0]["out"]
    return y.transpose(1, 0, 2).reshape(BATCH, SEQ, D)
```

```python
from contextlib import ExitStack

import numpy as np

import concourse.bass as bass
from concourse import mybir

BATCH, SEQ, D, CTX, HEADS = 16, 256, 128, 1601, 16
DH = D // HEADS
PAIRS = HEADS // 2
QTILES = SEQ // 128
TILES = BATCH * QTILES
CHUNK = 512
CHUNKS = BATCH * SEQ // CHUNK
EXPERTS, HID = 8, 64
GELU_TILES = EXPERTS * HID // 128
EPS = 1e-5
SCALE = float(DH) ** -0.5

KTILES = (CTX + 127) // 128
KEY0 = [min(128 * t, CTX - 128) for t in range(KTILES)]
REPEATED = 128 * (KTILES - 1) - KEY0[-1]
RUN = 401
RUN0 = [400 * i for i in range(4)]
KRUN = [(0, 401), (401, 400), (801, 400), (1201, 400)]

KPART = [0, 1, 2, 0, 1, 0]
QPART = [0, 0, 0, 1, 1, 2]
ROWS = 16 * len(KPART)
MROWS = ROWS + 3

GP = PAIRS // 2
STEPS = 2 * BATCH
UNITS = KTILES * GP
SUNITS = 2 * GP * QTILES * 2
Q_FIRST = -7
FFN_FIRST = 5
FIRST, LAST = Q_FIRST, FFN_FIRST + 4 * (CHUNKS - 1) + 3
LOOP0, PERIOD = 9, 4
TURNS = 4
STB, PB = 3, 8

ALU = mybir.AluOpType
ACT = mybir.ActivationFunctionType
AX = mybir.AxisListType
F32 = mybir.dt.float32
BF16 = mybir.dt.bfloat16


def scored(s):
    return UNITS * min(max(s, 0), STEPS)


def chunks_before(s, first):
    return min(max((s - first + 3) // 4, 0), CHUNKS)


def begins(s, first):
    return chunks_before(s + 1, first) > chunks_before(s, first)


def aux_kinds(s):
    b, middle, end, placed = s // 2, [], [], []
    if s % 2 == 0 and 0 <= b + 2 < BATCH:
        placed += [(4, [("K", 0)]), (9, [("K", 1)])]
    if s % 2 == 1 and 0 <= b + 1 < BATCH:
        placed += [(4, [("V", 0)]), (9, [("V", 1)])]
    if 0 <= s + 1 < STEPS:
        placed += [(1, [("T", 0)])]
    if 0 <= s + 2 < STEPS:
        middle = [("S", i) for i in range(SUNITS)]
    if s % 2 == 0 and 0 <= b - 1 < BATCH:
        end = [("D", 0)]
    if begins(s, Q_FIRST):
        placed += [(6, [("QT", 0)]), (12, [("QP", 0)])]
    if begins(s, FFN_FIRST):
        placed += [(8, [("FT", 0)]), (14, [("FL", 0)])]
    if begins(s - 1, FFN_FIRST):
        placed += [(6, [("FG", 0)]), (16, [("FH", 0), ("FH", 1), ("FH", 2)])]
    if begins(s - 2, FFN_FIRST):
        placed += [(12, [("FB", 0)]), (20, [("FB", 1)])]
    if begins(s - 3, FFN_FIRST):
        placed += [(12, [("FY", 0)]), (20, [("FY", 1)])]
    for place, units in sorted(placed):
        middle[place:place] = units
    return middle + end


def aux_before(s):
    return sum(len(aux_kinds(r)) for r in range(FIRST, s))


def unit_of(s, kind, i):
    return aux_before(s) + aux_kinds(s).index((kind, i))


SCALAR_UNITS = ("K", "T", "QT", "QP", "FT", "FL", "FG", "FH")


def order(s):
    units = aux_kinds(s)
    groups = []
    for n, (kind, i) in enumerate(units):
        if kind == "FH" and i > 0:
            groups[-1].append(("aux", n))
        else:
            groups.append([("aux", n)])
    gaps = [[] for _ in range(3 * KTILES)]
    for n, group in enumerate(groups):
        gaps[n * len(gaps) // len(groups)] += group
    events = []
    for quad in range(KTILES):
        gap = gaps[3 * quad:3 * quad + 3]
        scores = [("score", GP * quad + j) for j in range(GP)] if 0 <= s < STEPS else []
        copy = [("o_copy", 0)] if quad == 1 and 0 <= s - 1 < STEPS else []
        values = []
        if quad == 0 and 0 <= s - 1 < STEPS:
            values = [("value_before", UNITS - GP + j) for j in range(GP)]
        if quad > 0 and 0 <= s < STEPS:
            values = [("value", GP * (quad - 1) + j) for j in range(GP)]
        if scores:
            events += copy + gap[0] + scores[:2] + gap[1] + values + gap[2] + scores[2:]
        else:
            events += values + copy + gap[0] + gap[1] + gap[2]
    return events


class Step:

    def __init__(self, s, turn=None):
        self.s, self.turn = s, turn

    def at(self, count, ds=0):
        first = count(self.s + ds)
        if self.turn is None:
            return first
        grows = count(self.s + ds + PERIOD) - first
        for i in range(TURNS):
            assert count(self.s + ds + PERIOD * i) == first + i * grows
        return self.turn * grows + first if grows else first

    def back(self, ds):
        return Step(self.s + ds, self.turn)


def wait(eng, sem, value):
    if not isinstance(value, int) or value > 0:
        eng.wait_ge(sem, value)


def run_steps(eng, body):
    for s in range(FIRST, LOOP0):
        body(Step(s))
    with eng.Fori(0, TURNS) as turn:
        for u in range(PERIOD):
            body(Step(LOOP0 + u, turn))
    for s in range(LOOP0 + PERIOD * TURNS, LAST + 1):
        body(Step(s))


def flamingo_block(nc, x, ctx_t, wq, wk, wv, wd, bq, bk, bv, bd, g_attn, g_ffn,
                   gate_w, w1, ws1, w2, ws2, b1, bs1, b2s, route, ident_in, earlier_in, pick_in, out):
    with ExitStack() as ctx:
        def sb(name, shape, dt=F32):
            return ctx.enter_context(nc.sbuf_tensor(name, shape, dt))

        def sem(name):
            return ctx.enter_context(nc.semaphore(name))

        q_dram = nc.dram_tensor("q_dram", [3, 128, BATCH, 2 * SEQ], BF16, kind="Internal").ap()
        k_dram = nc.dram_tensor("k_dram", [2, 3, 128, CTX], BF16, kind="Internal").ap()
        m_dram = nc.dram_tensor("m_dram", [2, 3, 2 * GP, SEQ], BF16, kind="Internal").ap()
        o_dram = nc.dram_tensor("o_dram", [2, 128, 2 * SEQ], F32, kind="Internal").ap()

        st_ps = [ctx.enter_context(nc.psum_tensor(f"st_ps{i}", [128, 512], F32)) for i in range(STB)]
        o_ps = ctx.enter_context(nc.psum_tensor("o_ps", [128, 512], F32))
        aux_ps = [ctx.enter_context(nc.psum_tensor(f"aux_ps{i}", [128, 2, 512], F32)) for i in range(2)]

        wq_s, wk_s, wv_s, wd_s = (sb(n, [128, 128]) for n in ("wq_s", "wk_s", "wv_s", "wd_s"))
        bq_s, bk_s, gx_s, gf_s, route_s = (sb(n, [128, 1]) for n in ("bq_s", "bk_s", "gx_s", "gf_s", "route_s"))
        one, minus_half = sb("one", [128, 1]), sb("minus_half", [128, 4])
        tgx, tgf = sb("tgx", [128, 1]), sb("tgf", [128, 1])
        bv_s, bd_s = sb("bv_s", [128, 128]), sb("bd_s", [128, 128])
        ident, earlier = sb("ident", [128, 128]), sb("earlier", [128, EXPERTS, EXPERTS])
        pick = sb("pick", [EXPERTS, GELU_TILES, 128])
        gate_s, w1_s, ws1_s = sb("gate_s", [128, EXPERTS]), sb("w1_s", [128, EXPERTS * HID]), sb("ws1_s", [128, HID])
        w2_s, ws2_s = sb("w2_s", [128, GELU_TILES, 128]), sb("ws2_s", [HID, 128])
        b1_s, bs1_s, b2s_s = sb("b1_s", [128, GELU_TILES]), sb("bs1_s", [HID, 1]), sb("b2s_s", [EXPERTS + 1, 128])
        x_s = sb("x_s", [128, TILES, 128])
        norms = ("q", "f")
        stats = {w: sb(f"stats_{w}", [128, 4, 6]) for w in norms}
        mv = {w: sb(f"mv_{w}", [128, 4, 2]) for w in norms}
        eps = {w: sb(f"eps_{w}", [128, 4]) for w in norms}
        rstd = {w: sb(f"rstd_{w}", [128, 4]) for w in norms}
        xn = {w: sb(f"xn_{w}", [128, 4, 128]) for w in norms}
        xn_t = {w: sb(f"xn_t_{w}", [128, CHUNK]) for w in norms}
        q_t = sb("q_t", [128, CHUNK])
        q_parts = sb("q_parts", [128, 3, 2, 2, SEQ], BF16)
        kctx, vctx = sb("kctx", [128, CTX]), sb("vctx", [128, CTX])
        k_t = sb("k_t", [128, CTX])
        k_parts = sb("k_parts", [128, 3, CTX], BF16)
        k_op = [sb(f"k_op{i}", [MROWS, GP, CTX], BF16) for i in range(4)]
        q_op = [sb(f"q_op{i}", [MROWS, 2 * GP, SEQ], BF16) for i in range(4)]
        v_op = [sb(f"v_op{i}", [128, KTILES, PAIRS, 32]) for i in range(2)]
        probs = sb("probs", [128, PB, 512])
        run_max = sb("run_max", [128, QTILES * 2 * GP, 2])
        neg_max = sb("neg_max", [128, QTILES, 2 * GP])
        nm_t, nm_rest = sb("nm_t", [2 * GP, SEQ]), sb("nm_rest", [2 * GP, SEQ])
        nm_parts = sb("nm_parts", [2 * GP, 3, SEQ], BF16)
        o_s = [sb(f"o_s{i}", [128, 512]) for i in range(2)]
        num, den, attn = sb("num", [128, SEQ]), sb("den", [128, SEQ]), sb("attn", [128, SEQ])
        score = sb("score", [128, 4, EXPERTS])
        beats, ties = sb("beats", [128, 4, EXPERTS, EXPERTS]), sb("ties", [128, 4, EXPERTS, EXPERTS])
        rank, wsum, winv = sb("rank", [128, 4, EXPERTS]), sb("wsum", [128, 4]), sb("winv", [128, 4])
        g_tok = sb("g_tok", [128, 4, EXPERTS])
        g_t = sb("g_t", [EXPERTS + 1, CHUNK])
        hid = sb("hid", [128, GELU_TILES, CHUNK])
        hid_s = sb("hid_s", [HID, CHUNK])
        y_s = sb("y_s", [128, 4, 128])

        const_in, x_in, init, dve_init = sem("const_in"), sem("x_in"), sem("init"), sem("dve_init")
        tanh_done, xb_done = sem("tanh_done"), sem("xb_done")
        bn_seq, rstd_done, xn_ready = ({w: sem(f"{n}_{w}") for w in norms}
                                       for n in ("bn_seq", "rstd_done", "xn_ready"))
        bias_added, q_chain, q_written = sem("bias_added"), sem("q_chain"), sem("q_written")
        kctx_in, vctx_in = sem("kctx_in"), sem("vctx_in")
        op_in = [sem(f"op_in{i}") for i in range(4)]
        m_written, m_in = sem("m_written"), [sem(f"m_in{i}") for i in range(2)]
        k_written = sem("k_written")
        st_ready, exp_done, p_used = sem("st_ready"), sem("exp_done"), sem("p_used")
        aux_ready, aux_free = ([sem(f"{n}{i}") for i in range(2)] for n in ("aux_ready", "aux_free"))
        v_ready, nm_ready, m_chain, k_chain = sem("v_ready"), sem("nm_ready"), sem("m_chain"), sem("k_chain")
        o_copied, o_written, o_in = sem("o_copied"), sem("o_written"), [sem(f"o_in{i}") for i in range(2)]
        norm_seq = sem("norm_seq")
        gate_seq = sem("gate_seq")
        out_done = sem("out_done")

        consts = [(wq_s, wq), (wk_s, wk), (wv_s, wv), (wd_s, wd), (bq_s, bq), (bk_s, bk), (bv_s, bv), (bd_s, bd),
                  (gx_s, g_attn), (gf_s, g_ffn), (route_s, route), (ident, ident_in), (earlier, earlier_in),
                  (pick, pick_in), (gate_s, gate_w), (w1_s, w1), (ws1_s, ws1), (w2_s, w2), (ws2_s, ws2),
                  (b1_s, b1), (bs1_s, bs1), (b2s_s, b2s)]
        ALL_CONSTS = 16 * len(consts)
        GATE_OPS = 12
        INIT = 10

        def slot_of(st, n):
            return (aux_before(st.s) + n) % 2, st.at(lambda r: (aux_before(r) + n) // 2 + 1)

        def wait_taken(eng, st, kind, i=0):
            eng.wait_ge(aux_free[unit_of(st.s, kind, i) % 2], st.at(lambda r: unit_of(r, kind, i) // 2 + 1))

        def wait_all_taken(eng, st, units):
            last = {unit_of(st.s - back, kind, i) % 2: (back, kind, i) for back, kind, i in units}
            for back, kind, i in last.values():
                wait_taken(eng, st.back(-back), kind, i)

        block = ctx.enter_context(nc.Block())

        @block.sync
        def _(sp):
            for t in range(CHUNKS):
                sp.dma_start(x_s[:, 4 * t:4 * t + 4, :], x[:, 4 * t:4 * t + 4, :]).then_inc(x_in, 16)
            for dst, src in consts:
                sp.dma_start(dst[tuple([slice(None)] * len(src.shape))], src).then_inc(const_in, 16)
            sp.dma_start(kctx[:, :], ctx_t[0]).then_inc(kctx_in, 16)
            sp.dma_start(vctx[:, :], ctx_t[0]).then_inc(vctx_in, 16)

            registers = [ctx.enter_context(sp.register(f"sp_value{i}")) for i in range(20)]

            def held(v, i, top=None):
                if isinstance(v, int):
                    return v
                sp.reg_mov(registers[i], v)
                return registers[i] if top is None else sp.snap(registers[i], min_val=0, max_val=top)

            sp.wait_ge(init, INIT)

            def step(st):
                s = st.s
                b = s // 2
                used = []

                def value(count, ds=0, top=None):
                    used.append(0)
                    return held(st.at(count, ds), len(used) - 1, top)

                def at(i):
                    return i if isinstance(i, int) else bass.ds(i, 1)

                def held_slot(st, kind, i):
                    return unit_of(s, kind, i) % 2, value(lambda r: unit_of(r, kind, i) // 2 + 1)

                load_op = 0 <= s + 3 < STEPS
                store_o = 0 <= s - 1 < STEPS
                load_kctx = s % 2 == 0 and 0 <= b + 2 and b + 3 < BATCH
                load_vctx = s % 2 == 1 and 0 <= b + 1 and b + 2 < BATCH
                move_max = 0 <= s + 1 < STEPS
                store_k = s % 2 == 0 and 0 <= b + 2 < BATCH
                store_q = begins(s, Q_FIRST)
                store_y = begins(s - 3, FFN_FIRST)
                if load_op:
                    batch = value(lambda r: r // 2, 3, BATCH - 1)
                    scores_done = value(scored)
                    k_stored = value(lambda r: 48 * (r // 2 + 1), 3)
                    q_stored = value(lambda r: 48 * (r // 4 + 1), 3)
                if store_o:
                    o_ready = value(lambda r: r)
                    o_read = value(lambda r: 64 * ((r - 1) // 2))
                    o_stored = value(lambda r: 16 * r)
                    normalised = value(lambda r: 2 * ((r - 1) // 2)) if s % 2 == 1 else 0
                if load_kctx:
                    k_batch = value(lambda r: r // 2, 6, BATCH - 1)
                    taken = [held_slot(st, "K", i) for i in range(2)]
                if load_vctx:
                    v_batch = value(lambda r: r // 2, 4, BATCH - 1)
                    taken = [held_slot(st, "V", i) for i in range(2)]
                if move_max:
                    max_split, m_read = value(lambda r: 4 * (r + 1), 1), value(lambda r: 16 * (r // 2), 1)
                    m_stored = value(lambda r: 16 * (r + 1), 1)
                if store_k:
                    k_split = value(lambda r: 4 * (r // 2 + 1), 4)
                    loaded = [value(lambda r: 144 * ((r + d) // 4 + 1)) if s >= 0 else 0 for d in (0, 1)]

                if store_q:
                    q_split = value(lambda r: 8 * (chunks_before(r, Q_FIRST) + 1))
                    q_first = value(lambda r: 2 * chunks_before(r, Q_FIRST), 0, BATCH - 2)
                if store_y:
                    y_done = [held_slot(st, "FY", i) for i in range(2)]
                    y_first = value(lambda r: 4 * chunks_before(r, FFN_FIRST + 3), 0, TILES - 4)

                if load_op:
                    buf, g = (s + 3) % 4, (s + 3) % 2
                    wait(sp, st_ready, scores_done)
                    wait(sp, k_written, k_stored)
                    wait(sp, q_written, q_stored)
                    kd = k_dram[((s + 3) // 2) % 2].rearrange("n (a p) c -> (n a) p c", p=PAIRS)
                    qd = q_dram.rearrange("n (a p) b q -> n a p b q", p=PAIRS)
                    pairs = slice(GP * g, GP * g + GP)
                    for r0, r1 in ((0, 48), (48, 80), (80, 96)):
                        sp.dma_start(k_op[buf][r0:r1, :, :], kd[0:r1 - r0, pairs, :]).then_inc(op_in[buf], 16)
                    for r, part in enumerate(QPART):
                        src = qd[part, :, pairs, at(batch), :]
                        if not isinstance(batch, int):
                            src = src.rearrange("a p b q -> a p (b q)")
                        sp.dma_start(q_op[buf][16 * r:16 * r + 16, :, :].rearrange("r (p a) q -> r p (a q)", a=2),
                                     src).then_inc(op_in[buf], 16)
                if store_o:
                    h = (s - 1) % 2
                    wait(sp, o_copied, o_ready)
                    wait(sp, o_in[h], o_read)
                    sp.dma_start(o_dram[h], o_s[h][:, :]).then_inc(o_written, 16)
                    sp.wait_ge(o_written, o_stored)
                    wait(sp, norm_seq, normalised)
                    od = o_dram[h].rearrange("(j r) q -> j r q", r=32)
                    for side in range(2):
                        to = slice(64 * side + 32 * h, 64 * side + 32 * h + 32)
                        cols = slice(SEQ * side, SEQ * side + SEQ)
                        sp.dma_start(num[to, :], od[:, 8 * side:8 * side + 8, cols]).then_inc(o_in[h], 16)
                        sp.dma_start(den[to, :], od[:, 16:24, cols]).then_inc(o_in[h], 16)
                if load_kctx or load_vctx:
                    for slot, uses in taken:
                        sp.wait_ge(aux_ready[slot], uses)
                    dst, i, arrived = (kctx, k_batch, kctx_in) if load_kctx else (vctx, v_batch, vctx_in)
                    src = ctx_t[at(i)]
                    if not isinstance(i, int):
                        src = src.rearrange("o p c -> (o p) c")
                    sp.dma_start(dst[:, :], src).then_inc(arrived, 16)
                if move_max:
                    h = (s + 1) % 2
                    sp.wait_ge(m_chain, max_split)
                    wait(sp, m_in[h], m_read)
                    sp.dma_start(m_dram[h].rearrange("n h q -> h n q"), nm_parts[:, :, :]).then_inc(m_written, 16)
                    sp.wait_ge(m_written, m_stored)
                    sp.dma_start(q_op[(s + 1) % 4][ROWS:MROWS, :, :], m_dram[h]).then_inc(m_in[h], 16)
                if store_k:
                    sp.wait_ge(k_chain, k_split)
                    for d in (0, 1):
                        wait(sp, op_in[(s + d) % 4], loaded[d])
                    for part in range(3):
                        sp.dma_start(k_dram[(b + 2) % 2, part], k_parts[:, part, :]).then_inc(k_written, 16)
                if store_q:
                    sp.wait_ge(q_chain, q_split)
                    for part in range(3):
                        sp.dma_start(q_dram[part, :, bass.ds(q_first, 2), :],
                                     q_parts[:, part].rearrange("p b a q -> p b (a q)")).then_inc(q_written, 16)
                if store_y:
                    for slot, uses in y_done:
                        sp.wait_ge(aux_free[slot], uses)
                    sp.dma_start(out[:, bass.ds(y_first, 4), :], y_s[:, :, :]).then_inc(out_done, 16)
            run_steps(sp, step)
            sp.wait_ge(out_done, 16 * CHUNKS)

        @block.gpsimd
        def _(pool):
            for i in range(2):
                pool.memset(k_op[i][ROWS:MROWS, :, :], 1.0).then_inc(init, 1)

            def ones(like, rows_of=slice(0, 128)):
                factor = one[rows_of, :]
                while len(factor.shape) < len(like.shape):
                    factor = factor.unsqueeze(1)
                return factor.broadcast_to(list(like.shape))

            def q_split(st):
                wait_taken(pool, st, "QP")
                wait(pool, q_written, st.at(lambda r: 48 * chunks_before(r, Q_FIRST)))

                def wait_chain(n):
                    pool.wait_ge(q_chain, st.at(lambda r: 8 * chunks_before(r, Q_FIRST) + n))
                sides = [(slice(0, 64), 0), (slice(64, 128), 1)]
                qv = q_t[:, :].rearrange("p (b q) -> p b q", b=2)
                n = 0
                for part in range(3):
                    for rows, side in sides:
                        piece = q_parts[rows, part, :, side, :]
                        if part < 2:
                            pool.tensor_tensor(piece, qv[rows], ones(qv[rows], rows), ALU.mult).then_inc(q_chain, 1)
                            n += 1
                    if part < 2:
                        wait_chain(n)
                    for rows, side in sides:
                        if part == 0:
                            pool.tensor_tensor(qv[rows], qv[rows], q_parts[rows, 0, :, side, :],
                                               ALU.subtract).then_inc(q_chain, 1)
                            n += 1
                        if part == 1:
                            pool.tensor_tensor(q_parts[rows, 2, :, side, :], qv[rows], q_parts[rows, 1, :, side, :],
                                               ALU.subtract).then_inc(q_chain, 1)
                            n += 1
                    if part == 0:
                        wait_chain(n)
            def split3(chain, done, whole, parts, rest):
                pool.tensor_tensor(parts[0], whole, ones(whole, slice(0, whole.shape[0])), ALU.mult).then_inc(chain, 1)
                pool.wait_ge(chain, done + 1)
                pool.tensor_tensor(rest, whole, parts[0], ALU.subtract).then_inc(chain, 1)
                pool.wait_ge(chain, done + 2)
                pool.tensor_tensor(parts[1], rest, ones(rest, slice(0, rest.shape[0])), ALU.mult).then_inc(chain, 1)
                pool.wait_ge(chain, done + 3)
                pool.tensor_tensor(parts[2], rest, parts[1], ALU.subtract).then_inc(chain, 1)

            def inverse_root(st, w, first):
                pool.wait_ge(bn_seq[w], st.at(lambda r: 6 * (chunks_before(r, first) + 1)))
                pool.tensor_tensor(rstd[w][:, :], rstd[w][:, :], minus_half[:, :], ALU.pow).then_inc(rstd_done[w], 1)

            pool.wait_ge(init, INIT)

            def step(st):
                s = st.s
                if begins(s, FFN_FIRST):
                    inverse_root(st, "f", FFN_FIRST)
                if begins(s, Q_FIRST):
                    inverse_root(st, "q", Q_FIRST)
                if 0 <= s + 1 < STEPS:
                    wait_taken(pool, st, "T")
                    wait(pool, m_written, st.at(lambda r: 16 * r, 1))
                    split3(m_chain, st.at(lambda r: 4 * r, 1), nm_t[:, :],
                           [nm_parts[:, i, :] for i in range(3)], nm_rest[:, :])
                if begins(s, Q_FIRST):
                    for w, first in (("f", FFN_FIRST), ("q", Q_FIRST)):
                        if begins(s, first):
                            pool.wait_ge(rstd_done[w], st.at(lambda r: chunks_before(r, first) + 1))
                    wait(pool, k_chain, st.at(lambda r: 4 * min(max((r - 1) // 2 + 3, 0), BATCH)))
                    q_split(st)
                    pool.wait_ge(q_chain, st.at(lambda r: 8 * (chunks_before(r, Q_FIRST) + 1)))
                if s % 2 == 0 and 0 <= s // 2 + 2 < BATCH:
                    wait_all_taken(pool, st, [(0, "K", 0), (0, "K", 1)])
                    wait(pool, k_written, st.at(lambda r: 48 * (r // 2), 4))
                    split3(k_chain, st.at(lambda r: 4 * (r // 2), 4), k_t[:, :],
                           [k_parts[:, i, :] for i in range(3)], k_t[:, :])
            run_steps(pool, step)

        @block.scalar
        def _(act):
            act.wait_ge(const_in, ALL_CONSTS)
            act.activation(tgx[:, :], gx_s[:, :], ACT.Tanh).then_inc(tanh_done, 1)
            act.activation(tgf[:, :], gf_s[:, :], ACT.Tanh).then_inc(tanh_done, 1)

            def exponential(st, i):
                s = st.s
                act.wait_ge(st_ready, st.at(lambda r: scored(r) + i + 1))
                if scored(s) + i >= PB:
                    act.wait_ge(p_used, st.at(lambda r: scored(r) + i + 1 - PB))
                act.activation(probs[:, (scored(s) + i) % PB, :], st_ps[(i + s % 4) % STB][:, :], ACT.Exp,
                               scale=SCALE).then_inc(exp_done, 1)

            def aux_unit(st, n, kind, i):
                slot, uses = slot_of(st, n)
                bank = aux_ps[slot]
                act.wait_ge(aux_ready[slot], uses)
                if kind == "K":
                    if i == 0:
                        wait(act, k_chain, st.at(lambda r: 4 * (r // 2), 4))
                    for j in range(2):
                        k0, n_keys = KRUN[2 * i + j]
                        last = act.activation(k_t[:, k0:k0 + n_keys], bank[:, j, 0:n_keys], ACT.Identity,
                                              bias=bk_s[:, 0:1])
                elif kind == "T":
                    wait(act, m_chain, st.at(lambda r: 4 * r, 1))
                    last = act.activation(nm_t[:, :], bank[0:2 * GP, 0, 0:SEQ], ACT.Copy)
                elif kind in ("QT", "FT"):
                    last = act.activation(xn_t[kind[0].lower()][:, :], bank[:, 0, :], ACT.Copy)
                elif kind == "QP":
                    wait(act, q_chain, st.at(lambda r: 8 * chunks_before(r, Q_FIRST)))
                    last = act.activation(q_t[:, :], bank[:, 0, :], ACT.Identity, bias=bq_s[:, 0:1])
                elif kind == "FL":
                    last = act.activation(score[:, :, :], bank[:, 0, 0:4 * EXPERTS]
                                          .rearrange("p (t e) -> p t e", t=4), ACT.Exp, scale=-1.0)
                elif kind == "FG":
                    last = act.activation(g_t[0:EXPERTS, :], bank[0:EXPERTS, 0, :], ACT.Copy)
                elif kind == "FH" and i < 2:
                    for j in range(2):
                        m = 2 * i + j
                        last = act.activation(hid[:, m, :], bank[:, j, :], ACT.Gelu, bias=b1_s[:, m:m + 1])
                else:
                    last = act.activation(hid_s[:, :], bank[0:HID, 0, :], ACT.Gelu, bias=bs1_s[:, 0:1])
                last.then_inc(aux_free[slot], 1)

            def step(st):
                units = aux_kinds(st.s)
                for what, i in order(st.s):
                    if what == "score":
                        exponential(st, i)
                    elif what == "o_copy":
                        act.wait_ge(p_used, st.at(scored))
                        wait(act, o_written, st.at(lambda r: 16 * (r - 2)) if st.s > 2 else 0)
                        act.activation(o_s[(st.s - 1) % 2][:, :], o_ps[:, :], ACT.Copy).then_inc(o_copied, 1)
                    elif what == "aux" and units[i][0] in SCALAR_UNITS:
                        aux_unit(st, i, *units[i])
            run_steps(act, step)

        @block.tensor
        def _(pe):
            pe.wait_ge(const_in, ALL_CONSTS)

            pe.wait_ge(init, INIT)

            def aux_unit(st, n, kind, i):
                s = st.s
                slot_n, uses = slot_of(st, n)
                slot = aux_ps[slot_n]
                if aux_before(s) + n >= 2:
                    pe.wait_ge(aux_free[slot_n], uses - 1)
                if kind in ("QT", "FT"):
                    w, first = ("q", Q_FIRST) if kind == "QT" else ("f", FFN_FIRST)
                    pe.wait_ge(xn_ready[w], st.at(lambda r: 4 * (chunks_before(r, first) + 1)))
                    for t in range(4):
                        last = pe.transpose(slot[:, 0, 128 * t:128 * t + 128], xn[w][:, t, :], ident[:, :])
                elif kind == "QP":
                    wait_taken(pe, st, "QT")
                    last = pe.matmul(slot[:, 0, :], wq_s[:, :], xn_t["q"][:, :], start=True, stop=True)
                elif kind == "FL":
                    wait_taken(pe, st, "FT")
                    for t in range(4):
                        last = pe.matmul(slot[:, 0, 8 * t:8 * t + 8], xn_t["f"][:, 128 * t:128 * t + 128],
                                         gate_s[:, :], start=True, stop=True)
                elif kind == "FG":
                    pe.wait_ge(gate_seq, st.at(lambda r: GATE_OPS * (chunks_before(r, FFN_FIRST + 1) + 1)))
                    for t in range(4):
                        last = pe.transpose(slot[0:EXPERTS, 0, 128 * t:128 * t + 128], g_tok[:, t, :], ident[:, :])
                elif kind == "FH":
                    for j in range(2 if i < 2 else 1):
                        m = 2 * i + j
                        w, to = (w1_s[:, 128 * m:128 * m + 128], slot[:, j, :]) if i < 2 else \
                            (ws1_s[:, :], slot[0:HID, 0, :])
                        last = pe.matmul(to, w, xn_t["f"][:, :], start=True, stop=True)
                elif kind == "FB":
                    if i == 0:
                        wait_taken(pe, st.back(-1), "FG")
                    for j in range(2):
                        last = pe.matmul(slot[:, j, :], pick[:, 2 * i + j, :], g_t[0:EXPERTS, :],
                                         start=True, stop=True)
                elif kind == "FY":
                    if i == 0:
                        wait_all_taken(pe, st, [(2, "FH", 2), (1, "FB", 0), (1, "FB", 1)])
                    for t in range(2):
                        tok = slice(128 * (2 * i + t), 128 * (2 * i + t) + 128)
                        y = slot[:, 0, 128 * t:128 * t + 128]
                        for m in range(GELU_TILES):
                            pe.matmul(y, hid[:, m, tok], w2_s[:, m, :], start=(m == 0), stop=False)
                        pe.matmul(y, hid_s[:, tok], ws2_s[:, :], start=False, stop=False)
                        last = pe.matmul(y, g_t[:, tok], b2s_s[:, :], start=False, stop=True)
                elif kind == "K":
                    pe.wait_ge(kctx_in, st.at(lambda r: 16 * (r // 2 + 1), 4))
                    for j in range(2):
                        k0, n_keys = KRUN[2 * i + j]
                        last = pe.matmul(slot[:, j, 0:n_keys], wk_s[:, :], kctx[:, k0:k0 + n_keys],
                                         start=True, stop=True)
                elif kind == "V":
                    pe.wait_ge(vctx_in, st.at(lambda r: 16 * (r // 2 + 1), 2))
                    for t in range(8 * i, min(8 * i + 8, KTILES)):
                        last = pe.matmul(slot[:, t % 8 // 4, 128 * (t % 4):128 * (t % 4) + 128],
                                         vctx[:, KEY0[t]:KEY0[t] + 128], wv_s[:, :], start=True, stop=True)
                elif kind == "T":
                    pe.wait_ge(nm_ready, st.at(lambda r: r + 1, 1))
                    for t in range(QTILES):
                        last = pe.transpose(slot[0:2 * GP, 0, 128 * t:128 * t + 128], neg_max[:, t, :], ident[:, :])
                elif kind == "S":
                    buf = (s + 2) % 4
                    if i == 0:
                        pe.wait_ge(op_in[buf], st.at(lambda r: 144 * (r // 4 + 1), 2))
                    h, t, half = i // 4, i // 2 % 2, i % 2
                    for j in range(2):
                        k0 = RUN0[2 * half + j]
                        last = pe.matmul(slot[:, j, 0:RUN], q_op[buf][0:ROWS, h, 128 * t:128 * t + 128],
                                         k_op[buf][0:ROWS, h // 2, k0:k0 + RUN], start=True, stop=True)
                else:
                    pe.wait_ge(norm_seq, st.at(lambda r: 2 * (r // 2)))
                    for t in range(QTILES):
                        last = pe.matmul(slot[:, 0, 128 * t:128 * t + 128], attn[:, 128 * t:128 * t + 128],
                                         wd_s[:, :], start=True, stop=True)
                last.then_inc(aux_ready[slot_n], 1)

            def scores(st, i):
                s = st.s
                buf = s % 4
                if i == 0:
                    pe.wait_ge(m_in[s % 2], st.at(lambda r: 16 * (r // 2 + 1)))
                behind = 0 if i == 0 and s % 4 == 0 else i - STB + 1
                if scored(s) + behind > 0:
                    pe.wait_ge(exp_done, st.at(lambda r: scored(r) + behind))
                t, j = i // GP, i % GP
                pe.matmul(st_ps[(i + s % 4) % STB][:, :], k_op[buf][:, j, KEY0[t]:KEY0[t] + 128],
                          q_op[buf][:, 2 * j:2 * j + 2, :], start=True, stop=True).then_inc(st_ready, 1)

            def values(st, i):
                s = st.s
                t, j = i // GP, i % GP
                pe.wait_ge(exp_done, st.at(lambda r: scored(r) + i + 1))
                if i == 0:
                    pe.wait_ge(v_ready, st.at(lambda r: r // 2 + 1))
                    wait(pe, o_copied, st.at(lambda r: r))
                pair = GP * (s % 2) + j
                pe.matmul(o_ps[32 * j:32 * j + 32, :], v_op[s // 2 % 2][:, t, pair, :],
                          probs[:, (scored(s) + i) % PB, :], start=(t == 0), stop=(t == KTILES - 1)).then_inc(p_used, 1)

            def step(st):
                units = aux_kinds(st.s)
                for what, i in order(st.s):
                    if what == "score":
                        scores(st, i)
                    elif what == "aux":
                        aux_unit(st, i, *units[i])
                    elif what == "value":
                        values(st, i)
                    elif what == "value_before":
                        values(st.back(-1), i)
            run_steps(pe, step)

        @block.vector
        def _(dve):
            for i in range(2):
                dve.memset(v_op[i][:, :, :, 16:32], 1.0).then_inc(dve_init, 1)
            dve.memset(one[:, :], 1.0).then_inc(init, 1)
            dve.memset(minus_half[:, :], -0.5).then_inc(init, 1)
            dve.memset(q_parts[:, :, :, :, :], 0.0).then_inc(init, 1)
            dve.memset(g_t[:, :], 1.0).then_inc(init, 1)
            for i in (2, 3):
                dve.memset(k_op[i][ROWS:MROWS, :, :], 1.0).then_inc(init, 1)
            dve.wait_ge(dve_init, 2)
            for i in range(2):
                dve.memset(v_op[i][0:REPEATED, KTILES - 1, :, :], 0.0).then_inc(init, 1)

            dve.wait_ge(tanh_done, 2)
            dve.tensor_scalar(bd_s[:, :], bd_s[:, :], tgx[:, 0:1], None, ALU.mult).then_inc(xb_done, 1)
            dve.wait_ge(xb_done, 1)
            dve.wait_ge(x_in, 16 * CHUNKS)
            dve.wait_ge(init, INIT)

            def tile_of(first, t):
                if isinstance(first, int):
                    return x_s[:, first + t, :]
                return x_s[:, bass.ds(first + t, 1), :].rearrange("p o d -> p (o d)")

            def statistics(st, w, begin):
                chunk = lambda r: chunks_before(r, begin)
                seq = lambda k: dve.wait_ge(bn_seq[w], st.at(lambda r: 6 * chunk(r) + k))
                first = st.at(lambda r: 4 * chunk(r))
                for t in range(4):
                    dve.bn_stats(stats[w][:, t, :], tile_of(first, t)).then_inc(bn_seq[w], 1)
                seq(4)
                dve.memset(eps[w][:, :], EPS)
                for t in range(4):
                    last = dve.bn_aggr(mv[w][:, t, :], stats[w][:, t, :])
                last.then_inc(bn_seq[w], 1)
                seq(5)
                dve.tensor_tensor(rstd[w][:, :], mv[w][:, :, 1], eps[w][:, :], ALU.add).then_inc(bn_seq[w], 1)

            def normalise(st, w, begin):
                chunk = lambda r: chunks_before(r, begin)
                dve.wait_ge(rstd_done[w], st.at(lambda r: chunk(r) + 1))
                first = st.at(lambda r: 4 * chunk(r))
                for t in range(4):
                    dve.tensor_scalar(xn[w][:, t, :], tile_of(first, t), mv[w][:, t, 0:1], rstd[w][:, t:t + 1],
                                      ALU.subtract, ALU.mult).then_inc(xn_ready[w], 1)

            def add_bias(st):
                dve.wait_ge(xn_ready["q"], st.at(lambda r: 4 * (chunks_before(r, Q_FIRST) + 1)))
                first = st.at(lambda r: 4 * chunks_before(r, Q_FIRST))
                tiles = slice(first, first + 4) if isinstance(first, int) else bass.ds(first, 4)
                dve.tensor_tensor(x_s[:, tiles, :], x_s[:, tiles, :],
                                  bd_s[:, :].unsqueeze(1).broadcast_to([128, 4, 128]), ALU.add)\
                   .then_inc(bias_added, 1)

            def gate(st, k):
                before = lambda r: GATE_OPS * chunks_before(r, FFN_FIRST)
                if k == 0:
                    wait_taken(dve, st, "FL")
                else:
                    dve.wait_ge(gate_seq, st.at(lambda r: before(r) + k))
                square = [128, 4, EXPERTS, EXPERTS]
                other, own = score[:, :, :].unsqueeze(2).broadcast_to(square), \
                    score[:, :, :].unsqueeze(3).broadcast_to(square)
                if k == 0:
                    op = dve.tensor_scalar(score[:, :, :], score[:, :, :], 1.0, None, ALU.add)
                elif k == 1:
                    op = dve.reciprocal(score[:, :, :], score[:, :, :])
                elif k == 2:
                    op = dve.tensor_scalar(score[:, :, :], score[:, :, :], route_s[:, 0:1], None, ALU.mult)
                elif k == 3:
                    op = dve.tensor_tensor(beats[:, :, :, :], other, own, ALU.is_gt)
                elif k == 4:
                    op = dve.tensor_tensor(ties[:, :, :, :], other, own, ALU.is_equal)
                elif k == 5:
                    op = dve.tensor_tensor(ties[:, :, :, :], ties[:, :, :, :],
                                           earlier[:, :, :].unsqueeze(1).broadcast_to(square), ALU.mult)
                elif k == 6:
                    op = dve.tensor_tensor(beats[:, :, :, :], beats[:, :, :, :], ties[:, :, :, :], ALU.add)
                elif k == 7:
                    op = dve.tensor_reduce(rank[:, :, :], beats[:, :, :, :], AX.X, ALU.add)
                elif k == 8:
                    op = dve.scalar_tensor_tensor(out=rank[:, :, :], in0=rank[:, :, :], scalar=1.5,
                                                  in1=score[:, :, :], op0=ALU.is_lt, op1=ALU.mult)
                elif k == 9:
                    op = dve.tensor_reduce(wsum[:, :], rank[:, :, :], AX.X, ALU.add)
                elif k == 10:
                    op = dve.reciprocal(winv[:, :], wsum[:, :])
                else:
                    op = dve.tensor_tensor(g_tok[:, :, :], rank[:, :, :], winv[:, :].unsqueeze(2)
                                           .broadcast_to([128, 4, EXPERTS]), ALU.mult)
                op.then_inc(gate_seq, 1)

            def aux_unit(st, n, kind, i):
                s = st.s
                slot_n, uses = slot_of(st, n)
                slot = aux_ps[slot_n]
                dve.wait_ge(aux_ready[slot_n], uses)
                if kind == "V":
                    v = v_op[(s // 2 + 1) % 2]
                    if i == 0:
                        wait(dve, p_used, st.at(scored, -1))
                    for j in range(2):
                        t0 = 8 * i + 4 * j
                        nt = min(4, KTILES - t0)
                        src = slot[:, j, 0:128 * nt].rearrange("p (t m c) -> p t m c", t=nt, c=16)
                        bias = bv_s[:, :].rearrange("p (m c) -> p m c", c=16).unsqueeze(1)\
                            .broadcast_to([128, nt, PAIRS, 16])
                        last = dve.tensor_tensor(v[:, t0:t0 + nt, :, 0:16], src, bias, ALU.add)
                    last.then_inc(aux_free[slot_n], 1)
                    if i == 1:
                        dve.wait_ge(aux_free[slot_n], uses)
                        dve.memset(v[0:REPEATED, KTILES - 1, :, 0:16], 0.0).then_inc(v_ready, 1)
                elif kind == "FB":
                    if i == 0:
                        wait_all_taken(dve, st, [(1, "FH", 0), (1, "FH", 1)])
                    for j in range(2):
                        last = dve.tensor_tensor(hid[:, 2 * i + j, :], hid[:, 2 * i + j, :], slot[:, j, :], ALU.mult)
                    last.then_inc(aux_free[slot_n], 1)
                elif kind == "FY":
                    chunk = lambda r: chunks_before(r, FFN_FIRST + 3)
                    if i == 0:
                        wait(dve, out_done, st.at(lambda r: 16 * chunk(r)))
                    first = st.at(lambda r: 4 * chunk(r) + 2 * i)
                    tiles = slice(first, first + 2) if isinstance(first, int) else bass.ds(first, 2)
                    dve.scalar_tensor_tensor(out=y_s[:, 2 * i:2 * i + 2, :].rearrange("p t d -> p (t d)"),
                                             in0=slot[:, 0, 0:2 * 128], scalar=tgf[:, 0:1],
                                             in1=x_s[:, tiles, :].rearrange("p t d -> p (t d)"),
                                             op0=ALU.mult, op1=ALU.add).then_inc(aux_free[slot_n], 1)
                elif kind == "S":
                    if i == 0:
                        wait(dve, nm_ready, st.at(lambda r: r, 2))
                    h, t, half = i // 4, i // 2 % 2, i % 2
                    dve.tensor_reduce(run_max[:, 2 * GP * t + h, half:half + 1], slot[:, :, 0:RUN], AX.XY,
                                      ALU.max).then_inc(aux_free[slot_n], 1)
                    if i == SUNITS - 1:
                        dve.wait_ge(aux_free[slot_n], uses)
                        dve.tensor_reduce(neg_max[:, :, :].rearrange("p t h -> p (t h)"), run_max[:, :, :], AX.X,
                                          ALU.max, negate=True).then_inc(nm_ready, 1)
                else:
                    tiles = st.at(lambda r: r - 2)
                    tiles = bass.ds(tiles, 2) if not isinstance(tiles, int) else slice(tiles, tiles + 2)
                    dve.scalar_tensor_tensor(out=x_s[:, tiles, :].rearrange("p t d -> p (t d)"),
                                             in0=slot[:, 0, 0:2 * 128], scalar=tgx[:, 0:1],
                                             in1=x_s[:, tiles, :].rearrange("p t d -> p (t d)"),
                                             op0=ALU.mult, op1=ALU.add).then_inc(aux_free[slot_n], 1)

            def step(st):
                s = st.s
                units = aux_kinds(s)
                last = len(units) - (("D", 0) in units)
                for n in range(len(units) + 1):
                    if n == min(1, last) and begins(s, FFN_FIRST):
                        wait_taken(dve, st.back(-1), "D")
                        statistics(st, "f", FFN_FIRST)
                    if n == min(2, last) and begins(s, Q_FIRST):
                        statistics(st, "q", Q_FIRST)
                    if n == min(7, last):
                        if begins(s, Q_FIRST):
                            normalise(st, "q", Q_FIRST)
                        if begins(s, FFN_FIRST):
                            normalise(st, "f", FFN_FIRST)
                    if n == min(11, last) and begins(s, Q_FIRST):
                        add_bias(st)
                    if n == min(24, last) and s % 2 == 0 and 0 <= s // 2 - 1 < BATCH:
                        for h in range(2):
                            dve.wait_ge(o_in[h], st.at(lambda r: 64 * (r // 2)))
                        dve.reciprocal(den[:, :], den[:, :]).then_inc(norm_seq, 1)
                        dve.wait_ge(norm_seq, st.at(lambda r: 2 * (r // 2) - 1))
                        dve.tensor_tensor(attn[:, :], num[:, :], den[:, :], ALU.mult).then_inc(norm_seq, 1)
                    if n < len(units):
                        aux_unit(st, n, *units[n]) if units[n][0] not in SCALAR_UNITS else None
                    if begins(s, FFN_FIRST):
                        after = n - units.index(("FL", 0)) - 2
                        if 0 <= after < GATE_OPS and n < len(units):
                            gate(st, after)
                        if n == len(units):
                            for k in range(max(0, after), GATE_OPS):
                                gate(st, k)
            run_steps(dve, step)


def kernel(**inputs):
    import concourse.bacc as bacc
    from concourse.bass_utils import run_bass_kernel_spmd

    a = {n: np.asarray(v) for n, v in inputs.items()}

    def column(v):
        return v.reshape(-1, 1)

    def rows(v):
        return np.broadcast_to(v.reshape(1, -1), (128, v.size))

    sdp = np.arange(D).reshape(PAIRS, 2 * DH).T.reshape(-1)
    spd = np.arange(D).reshape(PAIRS, 2, DH).transpose(1, 0, 2).reshape(-1)
    earlier = np.tril(np.ones((EXPERTS, EXPERTS), np.float32), -1)
    pick = np.zeros((EXPERTS, GELU_TILES, 128), np.float32)
    for e in range(EXPERTS):
        pick[e, e // 2, HID * (e % 2):HID * (e % 2) + HID] = 1.0
    arrays = {
        "x": a["x"].reshape(TILES, 128, D).transpose(1, 0, 2),
        "ctx_t": a["ctx_1024"].transpose(0, 2, 1),
        "wq": a["L0_xattn_wq_w"][sdp].T, "wk": a["L0_xattn_wk_w"][sdp].T, "wv": a["L0_xattn_wv_w"].T,
        "wd": a["L0_xattn_dense_w"].T[spd],
        "bq": column(a["L0_xattn_wq_b"][sdp]), "bk": column(a["L0_xattn_wk_b"][sdp]),
        "bv": rows(a["L0_xattn_wv_b"]), "bd": rows(a["L0_xattn_dense_b"]),
        "g_attn": rows(a["g_xattn"]), "g_ffn": rows(a["g_ffn"]),
        "gate_w": a["L0_ffn_gate_W"], "w1": a["L0_ffn_W1"].transpose(1, 0, 2).reshape(D, EXPERTS * HID),
        "ws1": a["L0_ffn_Ws1"],
        "w2": a["L0_ffn_W2"].reshape(GELU_TILES, 128, D).transpose(1, 0, 2), "ws2": a["L0_ffn_Ws2"],
        "b1": a["L0_ffn_b1"].reshape(GELU_TILES, 128).T, "bs1": column(a["L0_ffn_bs1"]),
        "b2s": np.concatenate([a["L0_ffn_b2"], a["L0_ffn_bs2"].reshape(1, D)]),
        "route": rows(a["L0_ffn_route_scale"]),
        "ident_in": np.eye(128, dtype=np.float32),
        "earlier_in": np.broadcast_to(earlier, (128, EXPERTS, EXPERTS)),
        "pick_in": pick,
    }
    arrays = {n: np.ascontiguousarray(v) for n, v in arrays.items()}
    nc = bacc.Bacc("TRN2", target_bir_lowering=False, num_devices=1)
    args = [nc.dram_tensor(n, v.shape, mybir.dt.from_np(v.dtype), kind="ExternalInput").ap()
            for n, v in arrays.items()]
    out = nc.dram_tensor("out", (128, TILES, D), F32, kind="ExternalOutput").ap()
    flamingo_block(nc, *args, out)
    r = run_bass_kernel_spmd(nc, [arrays], core_ids=[0])
    y = r.results[0]["out"]
    return y.transpose(1, 0, 2).reshape(BATCH, SEQ, D)
```
